# Optimizing a Trainium2 kernel written in Bass

```python
import numpy as np
import jax
import jax.numpy as jnp

def _softmax(x, axis=-1):
    return jax.nn.softmax(x, axis=axis)

def _gelu(x):
    return jax.nn.gelu(x, approximate=True)

def _silu(x):
    return jax.nn.silu(x)

def _sigmoid(x):
    return jax.nn.sigmoid(x)

def _layernorm(x, axis=-1, eps=1e-05):
    m = jnp.mean(x, axis=axis, keepdims=True)
    v = jnp.var(x, axis=axis, keepdims=True)
    return (x - m) / jnp.sqrt(v + eps)

def _scatter_add(tgt, idx, src, axis=0):
    return tgt.at[idx].add(src)

def _segment_sum(src, seg, n):
    return jax.ops.segment_sum(src, seg, n)
kernel_name = 'mk_conv_preact_d2_conv_nhwc768_r4_8c146f'

def setup_inputs(seed: int=0):
    np.random.seed(seed)
    _w = jnp.asarray

    def _rec_inputs():
        import jax
        import jax.numpy as jnp
        _gk = jax.random.key(seed)
        x = -0.0001538 + 1 * jax.random.normal(jax.random.fold_in(_gk, 1), (8, 32, 32, 192), jnp.float32)
        return x
    x = _rec_inputs()

    def _L0_conv_setup():
        import jax, jax.numpy as jnp
        import numpy as np
        DIM = 192
        NUM_HEADS = 12
        key = jax.random.key(seed)
        k1, k2, k3 = jax.random.split(key, 3)
        x = jax.random.normal(k1, (8, 32, 32, DIM), dtype=jnp.float32)
        lim_qkv = float(np.sqrt(6.0 / (DIM + 3 * DIM)))
        lim_o = float(np.sqrt(6.0 / (DIM + DIM)))
        w_qkv = jax.random.uniform(k2, (DIM, 3 * DIM), jnp.float32, -lim_qkv, lim_qkv)
        w_o = jax.random.uniform(k3, (DIM, DIM), jnp.float32, -lim_o, lim_o)
        return {'x': x, 'w_qkv': w_qkv, 'w_o': w_o}
    _L0_conv_all = _L0_conv_setup()
    _L0_conv_in = {k: v for k, v in _L0_conv_all.items() if k in ('w_qkv', 'w_o')}
    del _L0_conv_all

    def _L1_conv_setup():
        import jax, jax.numpy as jnp
        import numpy as np
        DIM = 192
        NUM_BLOCKS = 4
        BLOCK = DIM // NUM_BLOCKS
        SCALE = 0.02

        def _block_mul(t, w):
            return jnp.einsum('...bd,bdk->...bk', t, w)
        key = jax.random.key(seed)
        ks = jax.random.split(key, 7)
        x = jax.random.normal(ks[0], (8, 16, 16, DIM), dtype=jnp.float32)
        w1 = SCALE * jax.random.normal(ks[1], (2, NUM_BLOCKS, BLOCK, BLOCK), dtype=jnp.float32)
        b1 = SCALE * jax.random.normal(ks[2], (2, NUM_BLOCKS, BLOCK), dtype=jnp.float32)
        w2 = SCALE * jax.random.normal(ks[3], (2, NUM_BLOCKS, BLOCK, BLOCK), dtype=jnp.float32)
        b2 = SCALE * jax.random.normal(ks[4], (2, NUM_BLOCKS, BLOCK), dtype=jnp.float32)
        lim = 1.0 / np.sqrt(DIM)
        bias_w = jax.random.uniform(ks[5], (DIM, DIM), minval=-lim, maxval=lim, dtype=jnp.float32)
        bias_b = jax.random.uniform(ks[6], (DIM,), minval=-lim, maxval=lim, dtype=jnp.float32)
        return {'x': x, 'w1': w1, 'b1': b1, 'w2': w2, 'b2': b2, 'bias_w': bias_w, 'bias_b': bias_b}
    _L1_conv_all = _L1_conv_setup()
    _L1_conv_in = {k: v for k, v in _L1_conv_all.items() if k in ('w1', 'b1', 'w2', 'b2', 'bias_w', 'bias_b')}
    del _L1_conv_all
    return {'x': x, 'L0_conv_w_qkv': _L0_conv_in['w_qkv'], 'L0_conv_w_o': _L0_conv_in['w_o'], 'L1_conv_w1': _L1_conv_in['w1'], 'L1_conv_b1': _L1_conv_in['b1'], 'L1_conv_w2': _L1_conv_in['w2'], 'L1_conv_b2': _L1_conv_in['b2'], 'L1_conv_bias_w': _L1_conv_in['bias_w'], 'L1_conv_bias_b': _L1_conv_in['bias_b']}

def reference(x, L0_conv_w_qkv, L0_conv_w_o, L1_conv_w1, L1_conv_b1, L1_conv_w2, L1_conv_b2, L1_conv_bias_w, L1_conv_bias_b):
    import jax
    import jax.numpy as jnp

    def _L0_conv_ref(x, w_qkv, w_o):
        import jax, jax.numpy as jnp
        import numpy as np
        DIM = 192
        NUM_HEADS = 12
        bs, h, w, c = x.shape
        n = h * w
        nh = NUM_HEADS
        hd = c // nh
        xt = x.reshape(bs, n, c)
        qkv = xt @ w_qkv
        qkv = qkv.reshape(bs, n, 3, nh, hd)
        qkv = jnp.transpose(qkv, (2, 0, 3, 1, 4))
        q, k, v = (qkv[0], qkv[1], qkv[2])
        scale = hd ** (-0.5)
        attn = jnp.einsum('bhqd,bhkd->bhqk', q, k) * scale
        attn = jax.nn.softmax(attn, axis=-1)
        out = jnp.einsum('bhqk,bhkd->bhqd', attn, v)
        out = out.swapaxes(1, 2).reshape(bs, n, c)
        out = out @ w_o
        side = int(n ** 0.5)
        return out.reshape(bs, side, side, -1)

    def _L1_conv_ref(x, w1, b1, w2, b2, bias_w, bias_b):
        import jax, jax.numpy as jnp
        import numpy as np
        DIM = 192
        NUM_BLOCKS = 4
        BLOCK = DIM // NUM_BLOCKS
        SCALE = 0.02

        def _block_mul(t, w):
            return jnp.einsum('...bd,bdk->...bk', t, w)
        B, H, W, C = x.shape
        nb = w1.shape[1]
        bs = C // nb
        bias = x @ bias_w.T + bias_b
        xb = x.reshape(B, H, W, nb, bs)
        xf = jnp.fft.rfftn(xb, axes=(1, 2), norm='ortho')
        xr, xi = (xf.real, xf.imag)
        r1 = jax.nn.relu(_block_mul(xr, w1[0]) - _block_mul(xi, w1[1]) + b1[0])
        i1 = jax.nn.relu(_block_mul(xr, w1[1]) + _block_mul(xi, w1[0]) + b1[1])
        r2 = _block_mul(r1, w2[0]) - _block_mul(i1, w2[1]) + b2[0]
        i2 = _block_mul(r2, w2[1]) + _block_mul(i1, w2[0]) + b2[1]
        xc = jax.lax.complex(r2, i2)
        out = jnp.fft.irfftn(xc, s=(H, W), axes=(1, 2), norm='ortho')
        out = out.reshape(B, H, W, C)
        return out + bias

    def _gn(v, G=32, eps=1e-05):
        B_, H_, W_, C_ = v.shape
        g = v.reshape(B_, H_, W_, G, C_ // G)
        m = jnp.mean(g, axis=(1, 2, 4), keepdims=True)
        s = jnp.var(g, axis=(1, 2, 4), keepdims=True)
        return ((g - m) / jnp.sqrt(s + eps)).reshape(v.shape)

    def _ln_c(v, eps=1e-06):
        m = jnp.mean(v, axis=-1, keepdims=True)
        s = jnp.var(v, axis=-1, keepdims=True)
        return (v - m) / jnp.sqrt(s + eps)

    def _ln_t(v, eps=1e-05):
        m = jnp.mean(v, axis=-1, keepdims=True)
        s = jnp.var(v, axis=-1, keepdims=True)
        return (v - m) / jnp.sqrt(s + eps)

    def _to_tokens(v):
        B_, H_, W_, C_ = v.shape
        return v.reshape(B_, H_ * W_, C_)

    def _from_tokens(t, like):
        return t.reshape(like.shape)
    x = x + _L0_conv_ref(_gn(x), L0_conv_w_qkv, L0_conv_w_o)
    x = x + _L1_conv_ref(_gn(x), L1_conv_w1, L1_conv_b1, L1_conv_w2, L1_conv_b2, L1_conv_bias_w, L1_conv_bias_b)
    return x

_drawn_inputs = setup_inputs


def setup_inputs(seed=0):
    import zlib

    import numpy as np

    out = dict(_drawn_inputs(seed))
    spreads = {}
    factors = {'L1_conv_w1': 3.392, 'L1_conv_b1': 8.0, 'L1_conv_w2': 2.739}
    for name, (base, spread) in spreads.items():
        noise = np.random.default_rng([zlib.crc32(name.encode()), seed]).standard_normal(out[name].shape)
        drawn = base * np.exp(spread * noise) if base else spread * noise
        out[name] = jnp.asarray(drawn.astype(out[name].dtype))
    for name, factor in factors.items():
        out[name] = (out[name] * factor).astype(out[name].dtype)
    return out
```

```python
from contextlib import ExitStack

import concourse.bass as bass
import numpy as np
from concourse import mybir

ALU = mybir.AluOpType
ACT = mybir.ActivationFunctionType
AX = mybir.AxisListType
F32 = mybir.dt.float32
BF16 = mybir.dt.bfloat16

P = 128
NB, SIDE, C = 8, 32, 192
TOK = SIDE * SIDE
NT = TOK // P
CH = C // 2
NH, HD = 12, 16
GH = 4
NG = NH // GH
STEPS = 16
HALF = 512
NBLK, BS = 4, 48
NS = SIDE // 2 + 1
NF = NS * SIDE
GROUP = 6
EPS = 1e-5
SCALE = HD ** -0.5
Q_PARTS = (0, 0, 0, 1, 1, 2)
K_PARTS = (0, 1, 2, 0, 1, 0)
KQ = HD * len(Q_PARTS)
TILES = GH * STEPS
MAX_TILES = [5] * 12 + [4] + [0] * 3

PREP_AT = {0: [("turn", 0), ("turn", 1)], 1: [("turn", 2), ("turn", 3)], 3: [("mean", 0)],
           4: [("var", 0)], 6: [("qk", 0)], 7: [("qk", 1)], 8: [("qk", 2)], 9: [("qk", 3)],
           10: [("qk", 4)], 11: [("qk", 5)], 12: [("v", 0), ("v", 1)], 13: [("v", 2), ("v", 3)]}
POST_AT = {8: [("proj", 0), ("proj", 1)], 9: [("proj", 2), ("proj", 3)],
           10: [("turn", 0), ("turn", 1)], 11: [("turn", 2), ("turn", 3)],
           13: [("mean", 0)], 14: [("var", 0)], 16: [("spread", 0)],
           19: [("dftw", 0), ("dftw", 1)], 20: [("dftw", 2), ("dftw", 3)],
           24: [("dfth", 0), ("dfth", 1)], 25: [("dfth", 2), ("dfth", 3)],
           26: [("dfth", 4), ("dfth", 5)],
           28: [("mix1", 0), ("mix1", 1)], 29: [("mix1", 2), ("mix1", 3)],
           30: [("mix1", 4), ("mix1", 5)], 31: [("mix1", 6), ("mix1", 7)],
           32: [("mix2", 0)], 33: [("mix2", 1), ("mix2", 2)], 34: [("mix2", 3), ("mix2", 4)],
           37: [("idfth", 0), ("idfth", 1)], 38: [("idfth", 2), ("idfth", 3)],
           42: [("idftw", 0), ("idftw", 1)], 43: [("idftw", 2), ("idftw", 3)]}


def in_order(at):
    return [piece for step in sorted(at) for piece in at[step]]


PREP, POST = in_order(PREP_AT), in_order(POST_AT)
N_PREP, N_POST = len(PREP), len(POST)
PREP_NO = {piece: n for n, piece in enumerate(PREP)}
POST_NO = {piece: n for n, piece in enumerate(POST)}


def w_slots():
    v_of = list(range(1, 16)) + [0, 16]
    out = {}
    for j in range(8):
        for part in range(2):
            for sl in range(2):
                out[j, part, sl] = (v_of[2 * j + sl], part == 1)
    out[7, 1, 1] = (16, False)
    return out


def constants():
    ang = 2 * np.pi / SIDE
    slots = w_slots()
    n = np.arange(SIDE)
    fw = np.zeros((P, P))
    iw = np.zeros((P, P))
    for (j, part, sl), (v, imag) in slots.items():
        weight = (1 if v in (0, 16) else 2) / SIDE
        for hl in range(4):
            row = (hl * 4 + part * 2 + sl) * 8 + j
            at = slice(hl * SIDE, (hl + 1) * SIDE)
            fw[at, row] = -np.sin(ang * v * n) if imag else np.cos(ang * v * n)
            iw[row, at] = -weight * np.sin(ang * v * n) if imag else weight * np.cos(ang * v * n)
    cos, sin = np.cos(ang * np.outer(n, n)), np.sin(ang * np.outer(n, n))
    fh = np.zeros((SIDE, 2, 2, 2, 2, SIDE))
    fh7 = np.zeros((SIDE, 2, 2, 2, 3, SIDE))
    ih = np.zeros((2, 2, SIDE, SIDE, 2, 2))
    ih7a = np.zeros((2, 2, SIDE, SIDE, 2, 2))
    ih7b = np.zeros((2, 2, SIDE, SIDE, 2, 2))
    for sl in range(2):
        fh[:, 0, sl, 0, sl] = cos
        fh[:, 1, sl, 0, sl] = sin
        fh[:, 0, sl, 1, sl] = -sin
        fh[:, 1, sl, 1, sl] = cos
        ih[0, sl, :, :, 0, sl] = cos
        ih[1, sl, :, :, 0, sl] = -sin
        ih[0, sl, :, :, 1, sl] = sin
        ih[1, sl, :, :, 1, sl] = cos
    fh7[:, :, 0, :, 0] = fh[:, :, 0, :, 0]
    for part, sl, to in ((0, 1, 1), (1, 1, 2)):
        fh7[:, part, sl, 0, to] = cos
        fh7[:, part, sl, 1, to] = -sin
    ih7a[:, 0] = ih[:, 0]
    ih7a[0, 1, :, :, 0, 1] = cos
    ih7a[1, 1, :, :, 0, 1] = -sin
    ih7b_rows = np.zeros((2, SIDE, SIDE, 2, 2))
    ih7b_rows[0, :, :, 1, 1] = cos
    ih7b_rows[1, :, :, 1, 1] = -sin
    ih7b = np.concatenate([ih7b_rows.reshape(64, P), np.zeros((64, P))])
    groups = np.zeros((P, CH))
    groups[:CH] = np.kron(np.eye(CH // GROUP), np.full((GROUP, GROUP), 1 / GROUP))
    sign = np.ones((P, 1))
    sign[BS:CH] = -1
    parts = {"ident": np.eye(P), "fw": fw, "iw": iw, "fh": fh.reshape(P, P) / SIDE,
             "fh7": fh7.reshape(P, C) / SIDE, "ih": ih.reshape(P, P), "ih7a": ih7a.reshape(P, P),
             "ih7b": ih7b, "groups": groups, "sign": sign}
    where, at = {}, 0
    for name, a in parts.items():
        where[name] = (at, a.shape[1])
        at += a.shape[1]
    return where, np.concatenate(list(parts.values()), axis=1).astype(np.float32)


def build(nc, consts, x, w_qkv, w_o, w1, b1, w2, b2, bias_w, bias_b, out):
    where, _ = constants()
    n_const = consts.shape[1]
    ctx = ExitStack()
    with ctx:
        def sb(name, shape, dt=F32):
            return ctx.enter_context(nc.sbuf_tensor(name, shape, dt))

        def bank(name, n=1):
            return ctx.enter_context(nc.psum_tensor(name, [P, n, HALF], F32))

        def sem(name):
            return ctx.enter_context(nc.semaphore(name))

        cst = sb("cst", [P, n_const])
        wv = sb("wv", [CH, 2, C])
        w_qk = sb("w_qk", [CH, 2, 2 * C])
        wo = sb("wo", [CH, 2, C])
        bias_t = sb("bias_t", [CH, 2, C])
        bias_all = sb("bias_all", [P, C])
        mix_a = sb("mix_a", [CH, NBLK, CH])
        mix_a_bias = sb("mix_a_bias", [CH, NBLK])
        mix_b = sb("mix_b", [CH, NBLK, CH])
        mix_b_bias_in = sb("mix_b_bias_in", [BS, 2, NBLK])
        mix_b_bias = sb("mix_b_bias", [P, 2 * C])

        def const(name, rows=P):
            at, n = where[name]
            return cst[0:rows, at:at + n]

        ident = const("ident")

        x_in = sb("x_in", [P, NT, C])
        xt = sb("xt", [CH, 2, TOK])
        qk_parts = sb("qk_parts", [P, 3, 3, TOK], BF16)
        rest = sb("rest", [P, 2, HALF])
        q_stack = sb("q_stack", [KQ + 2, NH, TOK], BF16)
        k_stack = sb("k_stack", [KQ + 2, NH, TOK], BF16)
        v_new = sb("v_new", [P, NT, C])
        v_aug = sb("v_aug", [P, NG, NT, GH, 32])
        stats = sb("stats", [CH, 2, 2, 2, 6])
        mean_var = sb("mean_var", [CH, 2, 2, 2])
        calc = sb("calc", [CH, 2, 12, 2])
        row_max = sb("row_max", [P, TILES])
        neg_max = sb("neg_max", [P, GH * NT])
        shift = sb("shift", [GH * NT, 2, P], BF16)
        probs = sb("probs", [P, 2 * GH, HALF])
        o_raw = sb("o_raw", [P, TOK])
        sums = sb("sums", [P, SIDE])
        sums_inv = sb("sums_inv", [P, SIDE])
        inv_all = sb("inv_all", [P, TOK])
        o_t = sb("o_t", [CH, 2, TOK])
        x1 = sb("x1", [P, NT, C])
        xt1 = sb("xt1", [CH, 2, TOK])
        affine = sb("affine", [P, 2, C])
        tok_n = sb("tok_n", [P, NT, C])
        rows_a = sb("rows_a", [P, NT, C])
        rows_b = sb("rows_b", [P, NT + 1, C])
        spec_a = sb("spec_a", [CH, NBLK * NF])
        spec_b = sb("spec_b", [P, NBLK * NF])

        spec = spec_a[:, :].rearrange("p (c r f) -> p c r f", c=2, r=2)
        hidden = spec_a[:, :].rearrange("p (b f) -> p b f", b=NBLK)
        spec_st = spec_b[0:CH, :].rearrange("p (b f) -> p b f", b=NBLK)
        mixed = spec_b[:, 0:5 * 2 * C].rearrange("p (t n) -> p t n", t=5)

        setup_at = 0

        def setup_tile(rows, *shape):
            nonlocal setup_at
            n = int(np.prod(shape))
            flat = rows_a[:, :, :].rearrange("p t n -> p (t n)")[0:rows, setup_at:setup_at + n]
            setup_at += n
            return flat.rearrange("p (a b) -> p a b", a=shape[0])

        bias_rows = setup_tile(CH, 2, C)
        mix_b_re = setup_tile(CH, NBLK, BS)
        mix_b_t = setup_tile(BS, NBLK, CH)
        mix_b_w1 = setup_tile(BS, NBLK, BS)
        mix_b_w0 = setup_tile(CH, NBLK, BS)
        w_raw = xt1[:, :, 0:2 * C]

        scores = bank("scores", 3)
        max_tiles = bank("max_tiles", 2)
        o_acc = bank("o_acc")
        prep_bank = bank("prep_bank")
        post_bank = bank("post_bank")

        x_loaded = sem("x_loaded")
        x1_loaded = sem("x1_loaded")
        weights_loaded = sem("weights_loaded")
        cleared = sem("cleared")
        qk_weights = sem("qk_weights")
        setup_made = sem("setup_made")
        setup_taken = sem("setup_taken")
        prep_made = sem("prep_made")
        prep_taken = sem("prep_taken")
        post_made = sem("post_made")
        post_taken = sem("post_taken")
        stats_done = [sem("prep_stats"), sem("post_stats")]
        calc_done = [sem("prep_calc"), sem("post_calc")]
        normed = [sem("prep_normed"), sem("post_normed")]
        part0_done = sem("part0_done")
        part1_done = sem("part1_done")
        part2_done = sem("part2_done")
        stacked = [sem(f"stacked{g}") for g in range(NG)]
        v_ready = sem("v_ready")
        scores_made = sem("scores_made")
        probs_made = sem("probs_made")
        pv_made = sem("pv_made")
        max_made = sem("max_made")
        max_taken = sem("max_taken")
        neg_max_done = sem("neg_max_done")
        shift_turned = sem("shift_turned")
        shift_split = sem("shift_split")
        shift_in = sem("shift_in")
        o_out = sem("o_out")
        sums_in = sem("sums_in")
        sums_inverted = sem("sums_inverted")
        inv_in = sem("inv_in")
        inv_spread = sem("inv_spread")
        o_normed = sem("o_normed")
        o_packed = sem("o_packed")
        tokens_done = sem("tokens_done")
        rows_in = sem("rows_in")
        spec_in = [sem("spec_in0"), sem("spec_in1")]
        mixed_in = sem("mixed_in")
        lines_in = sem("lines_in")
        stored = sem("stored")
        waits_alone = sem("waits_alone")

        def after(eng, s, count):
            if not isinstance(count, int) or count > 0:
                eng.wait_ge(s, count)

        def alone(eng):
            eng.sem_inc(waits_alone, 1)

        def batches(eng, prologue, body, tail):
            prologue()
            body(0, True, False)
            body(1, True, True)
            with eng.Fori(2, NB - 2) as b:
                body(b, True, True)
            body(NB - 2, True, True)
            body(NB - 1, False, True)
            tail()

        def image(dram, b):
            return dram[bass.ds(b, 1)].rearrange("o h w c -> (o h w) c").rearrange(
                "(t p) c -> p t c", p=P)

        PREP_LAST, POST_LAST = N_PREP, N_POST
        CALCS = 10
        block = ctx.enter_context(nc.Block())

        @block.sync
        def _(sp):
            def load_x(b):
                after(sp, prep_made, N_PREP * (b - 1) + PREP_NO["turn", 3] + 1)
                sp.dma_start(x_in[:, :, :], image(x, b)).then_inc(x_loaded, 16)

            def load_residual(b):
                after(sp, post_taken, N_POST * b)
                sp.dma_start(x1[:, :, :], image(x, b)).then_inc(x1_loaded, 16)

            def stack(b, g, which):
                after(sp, part2_done, 6 * b + 6)
                alone(sp)
                after(sp, scores_made, TILES * (NG * (b - 1) + g + 1))
                to, parts = ((q_stack, Q_PARTS), (k_stack, K_PARTS))[which]
                group = NG * which + g
                for n, part in enumerate(parts):
                    sp.dma_start(to[n * HD:(n + 1) * HD, GH * g:GH * (g + 1), :],
                                 qk_parts[64 * (group % 2):64 * (group % 2 + 1), part, group // 2, :]
                                 ).then_inc(stacked[g], 16)

            def shifts(b, g):
                slot = NG * b + g
                after(sp, shift_split, 2 * slot + 2)
                for n in range(2):
                    sp.dma_start(q_stack[KQ + n:KQ + n + 1, GH * g:GH * (g + 1), :],
                                 shift[:, n, :]).then_inc(shift_in, 16)

            def sums_down(slot):
                after(sp, o_out, 2 * slot + 2)
                alone(sp)
                after(sp, sums_inverted, slot)
                for h in range(GH):
                    sp.dma_start(sums[32 * h:32 * (h + 1), :],
                                 o_raw[32 * h + HD:32 * h + HD + 1, :]).then_inc(sums_in, 16)

            def sums_back(slot):
                after(sp, sums_inverted, slot + 1)
                alone(sp)
                after(sp, o_normed, slot)
                for h in range(GH):
                    sp.dma_start(inv_all[32 * h:32 * h + 1, :],
                                 sums_inv[32 * h:32 * (h + 1), :]).then_inc(inv_in, 16)

            def pack(b, g):
                after(sp, o_normed, NG * b + g + 1)
                alone(sp)
                after(sp, post_made, N_POST * (b - 1) + POST_NO["proj", 3] + 1)
                for h in range(GH):
                    head = GH * g + h
                    sp.dma_start(o_t[HD * (head % 6):HD * (head % 6 + 1), head // 6, :],
                                 o_raw[32 * h:32 * h + HD, :]).then_inc(o_packed, 16)

            def regroup_rows(b, k):
                after(sp, post_taken, N_POST * b + POST_NO["dftw", k] + 1)
                for t in (2 * k, 2 * k + 1):
                    sp.dma_start(rows_b[HD * t:HD * (t + 1), 0:NT, :],
                                 rows_a[:, t, :]).then_inc(rows_in, 16)

            def stack_spectrum(b, chunk):
                after(sp, post_taken, N_POST * b + POST_NO["dfth", 3 * chunk + 2] + 1)
                for half in range(2):
                    for part in range(2):
                        sp.dma_start(spec_st[BS * part:BS * (part + 1), 2 * chunk + half, :],
                                     spec[BS * half:BS * (half + 1), chunk, part, :]
                                     ).then_inc(spec_in[chunk], 16)

            def regroup_mixed(b):
                after(sp, post_taken, N_POST * b + POST_NO["mix2", 4] + 1)
                for part in range(2):
                    cols = slice(C * part, C * (part + 1))
                    for half in range(2):
                        sp.dma_start(rows_b[64 * part:64 * (part + 1), half:NT:2, :],
                                     mixed[64 * half:64 * (half + 1), 0:4, cols]
                                     ).then_inc(mixed_in, 16)
                    sp.dma_start(rows_b[SIDE * part:SIDE * (part + 1), NT, :],
                                 mixed[0:SIDE, 4, cols]).then_inc(mixed_in, 16)

            def regroup_lines(b):
                after(sp, post_taken, N_POST * b + POST_NO["idfth", 3] + 1)
                for t in range(NT):
                    sp.dma_start(rows_b[:, t, :],
                                 rows_a[HD * t:HD * (t + 1), 0:NT, :]).then_inc(lines_in, 16)

            def store(b):
                after(sp, post_taken, N_POST * b + N_POST)
                sp.dma_start(image(out, b), tok_n[:, :, :]).then_inc(stored, 16)

            def prologue():
                sp.dma_start(x_in[:, :, :], image(x, 0)).then_inc(x_loaded, 16)
                loads = [
                    (cst[:, :], consts),
                    (w_raw[:, :, :], w_qkv[:, 0:2 * C].rearrange("(c p) n -> p c n", p=CH)),
                    (wv[:, :, :], w_qkv[:, 2 * C:3 * C].rearrange("(c p) n -> p c n", p=CH)),
                    (wo[:, :, :], w_o.rearrange("(c p) n -> p c n", p=CH)),
                    (bias_rows[:, :, :], bias_w.rearrange("(c p) n -> p c n", p=CH)),
                    (bias_all[:, :], bias_b.rearrange("(o n) -> o n", o=1).partition_broadcast(P)),
                    (mix_a[0:BS, :, 0:BS], w1[0].rearrange("b d k -> d b k")),
                    (mix_a[0:BS, :, BS:CH], w1[1].rearrange("b d k -> d b k")),
                    (mix_a[BS:CH, :, 0:BS], w1[1].rearrange("b d k -> d b k")),
                    (mix_a[BS:CH, :, BS:CH], w1[0].rearrange("b d k -> d b k")),
                    (mix_b_re[0:BS, :, :], w2[0].rearrange("b d k -> d b k")),
                    (mix_b_re[BS:CH, :, :], w2[1].rearrange("b d k -> d b k")),
                    (mix_b_w1[:, :, :], w2[1].rearrange("b d k -> d b k")),
                    (mix_a_bias[0:BS, :], b1[0].rearrange("b k -> k b")),
                    (mix_a_bias[BS:CH, :], b1[1].rearrange("b k -> k b")),
                    (mix_b_bias_in[:, 0, :], b2[0].rearrange("b k -> k b")),
                    (mix_b_bias_in[:, 1, :], b2[1].rearrange("b k -> k b")),
                ]
                for to, src in loads:
                    sp.dma_start(to, src, allow_slow_non_contiguous=True).then_inc(weights_loaded, 16)
                after(sp, cleared, 1)
                sp.dma_start(mix_b_w0[BS:CH, :, :],
                             w2[0].rearrange("b d k -> d b k")).then_inc(weights_loaded, 16)
                load_x(1)
                for g in range(NG):
                    stack(0, g, 0)
                    stack(0, g, 1)
                shifts(0, 0)

            def body(b, prep, post):
                for u in range(NG * STEPS):
                    g, s = divmod(u, STEPS)
                    slot = NG * b + g
                    first = isinstance(b, int) and b == 0
                    before = not (first and g == 0)
                    if u == 0 and post:
                        load_residual(b - 1)
                    if s == 1:
                        if before:
                            sums_down(slot - 1)
                        if g == 0 and not first:
                            stack(b, 2, 0)
                        if g > 0 and prep:
                            stack(b + 1, g - 1, 0)
                    if s == 4:
                        if before:
                            sums_back(slot - 1)
                        if g == 0 and not first:
                            stack(b, 2, 1)
                        if g > 0 and prep:
                            stack(b + 1, g - 1, 1)
                    if u == 2 and prep and (not isinstance(b, int) or b + 2 < NB):
                        load_x(b + 2)
                    if s == 7 and before:
                        if g == 0:
                            pack(b - 1, NG - 1)
                        else:
                            pack(b, g - 1)
                    if s == 14 and (prep or g < NG - 1):
                        if g < NG - 1:
                            shifts(b, g + 1)
                        else:
                            shifts(b + 1, 0)
                    if post:
                        for kind, k in POST_AT.get(u, []):
                            if kind == "dftw":
                                regroup_rows(b - 1, k)
                            if kind == "dfth" and k % 3 == 2:
                                stack_spectrum(b - 1, k // 3)
                            if kind == "mix2" and k == 4:
                                regroup_mixed(b - 1)
                            if kind == "idfth" and k == 3:
                                regroup_lines(b - 1)
                            if kind == "idftw" and k == 3:
                                store(b - 1)

            def tail():
                b, slot = NB - 1, NG * NB - 1
                load_residual(b)
                sums_down(slot)
                sums_back(slot)
                pack(b, NG - 1)
                for k in range(4):
                    regroup_rows(b, k)
                stack_spectrum(b, 0)
                stack_spectrum(b, 1)
                regroup_mixed(b)
                regroup_lines(b)
                store(b)
                sp.wait_ge(stored, 16 * NB)

            batches(sp, prologue, body, tail)

        @block.gpsimd
        def _(pool):
            def moments(which, b, made, taken, no):
                q = calc[:, which]
                done = calc_done[which]
                mean, var = mean_var[:, which, :, 0], mean_var[:, which, :, 1]
                after(pool, taken, made + no["mean", 0] + 1)
                nc.gpsimd.tensor_tensor(q[:, 1, :], mean, q[:, 0, :], ALU.subtract).then_inc(done, 1)
                pool.wait_ge(done, CALCS * b + 1)
                nc.gpsimd.tensor_tensor(q[:, 2, :], q[:, 1, :], q[:, 1, :], ALU.mult).then_inc(done, 1)
                pool.wait_ge(done, CALCS * b + 2)
                nc.gpsimd.tensor_tensor(q[:, 3, :], q[:, 2, :], var, ALU.add).then_inc(done, 1)

            def inverse_std(which, b, made, taken, no):
                q = calc[:, which]
                done = calc_done[which]
                after(pool, taken, made + no["var", 0] + 1)
                alone(pool)
                nc.gpsimd.tensor_scalar(q[:, 5, :], q[:, 4, :], EPS, None, ALU.add).then_inc(done, 1)
                pool.wait_ge(done, CALCS * b + 4)
                nc.gpsimd.tensor_tensor(q[:, 6, :], q[:, 5, :], q[:, 11, :], ALU.pow).then_inc(done, 1)
                pool.wait_ge(done, CALCS * b + 5)
                nc.gpsimd.tensor_tensor(q[:, 7, :], q[:, 6, :], q[:, 6, :], ALU.mult).then_inc(done, 1)
                pool.wait_ge(done, CALCS * b + 6)
                nc.gpsimd.tensor_tensor(q[:, 7, :], q[:, 7, :], q[:, 5, :], ALU.mult).then_inc(done, 1)
                pool.wait_ge(done, CALCS * b + 7)
                alone(pool)
                nc.gpsimd.tensor_scalar(q[:, 7, :], q[:, 7, :], -0.5, 1.5, ALU.mult,
                                        ALU.add).then_inc(done, 1)
                pool.wait_ge(done, CALCS * b + 8)
                nc.gpsimd.tensor_tensor(q[:, 8, :], q[:, 6, :], q[:, 7, :], ALU.mult).then_inc(done, 1)
                pool.wait_ge(done, CALCS * b + 9)
                nc.gpsimd.tensor_tensor(q[:, 9, :], q[:, 0, :], q[:, 8, :], ALU.mult).then_inc(done, 1)

            def last_part(b, k):
                pool.wait_ge(part1_done, 6 * b + k + 1)
                cols = slice(HALF * (k % 2), HALF * (k % 2 + 1))
                nc.gpsimd.tensor_tensor(qk_parts[:, 2, k // 2, cols], rest[:, k % 2, :],
                                        qk_parts[:, 1, k // 2, cols], ALU.subtract
                                        ).then_inc(part2_done, 1)

            def place_v(b, g):
                after(pool, prep_taken, N_PREP * b + PREP_NO["v", 3] + 1)
                after(pool, pv_made, STEPS * (NG * (b - 1) + g + 1))
                alone(pool)
                nc.gpsimd.tensor_copy(
                    v_aug[:, g, :, :, 0:HD],
                    v_new[:, :, GH * HD * g:GH * HD * (g + 1)].rearrange("p t (h d) -> p t h d", h=GH)
                ).then_inc(v_ready, 1)

            def normalise_o(slot):
                pool.wait_ge(inv_spread, slot + 1)
                nc.gpsimd.tensor_tensor(o_raw[:, :], o_raw[:, :], inv_all[:, :],
                                        ALU.mult).then_inc(o_normed, 1)

            def normalise_tokens(b):
                after(pool, stored, 16 * b)
                pool.wait_ge(post_taken, N_POST * b + POST_NO["spread", 0] + 1)
                for half in range(2):
                    t = slice(4 * half, 4 * half + 4)
                    nc.gpsimd.tensor_tensor(tok_n[:, t, :], x1[:, t, :],
                                            affine[:, 0:1, :].broadcast_to([P, 4, C]),
                                            ALU.mult).then_inc(tokens_done, 1)
                    pool.wait_ge(tokens_done, 6 * b + 2 * half + 1)
                    nc.gpsimd.tensor_tensor(tok_n[:, t, :], tok_n[:, t, :],
                                            affine[:, 1:2, :].broadcast_to([P, 4, C]),
                                            ALU.subtract).then_inc(tokens_done, 1)
                for half in range(2):
                    t = slice(4 * half, 4 * half + 4)
                    nc.gpsimd.tensor_tensor(x1[:, t, :], x1[:, t, :],
                                            bias_all[:, :].unsqueeze(1).broadcast_to([P, 4, C]),
                                            ALU.add).then_inc(tokens_done, 1)

            def prep_piece(b, kind, k):
                if kind == "mean":
                    moments(0, b, N_PREP * b, prep_taken, PREP_NO)
                if kind == "var":
                    inverse_std(0, b, N_PREP * b, prep_taken, PREP_NO)
                if kind == "qk":
                    last_part(b, k)

            def post_piece(b, kind, k):
                if kind == "mean":
                    moments(1, b, N_POST * b, post_taken, POST_NO)
                if kind == "var":
                    inverse_std(1, b, N_POST * b, post_taken, POST_NO)
                if kind == "spread":
                    normalise_tokens(b)

            def prologue():
                nc.gpsimd.memset(mix_b_w0[:, :, :], 0.0).then_inc(cleared, 1)
                nc.gpsimd.memset(calc[:, :, 11, :], -0.5).then_inc(cleared, 1)
                nc.gpsimd.memset(inv_all[:, :], 0.0).then_inc(cleared, 1)
                nc.gpsimd.memset(rows_b[:, NT, :], 0.0).then_inc(cleared, 1)
                nc.gpsimd.memset(v_aug[:, :, :, :, :], 0.0).then_inc(cleared, 1)
                pool.wait_ge(cleared, 5)
                nc.gpsimd.memset(v_aug[:, :, :, :, HD:HD + 1], 1.0).then_inc(cleared, 1)
                pool.wait_ge(weights_loaded, 16 * 18)
                for c in range(2):
                    for group in range(2 * NG):
                        src = w_raw[:, c, 64 * group:64 * (group + 1)]
                        nc.gpsimd.tensor_copy(
                            w_qk[:, c, 64 * group:64 * (group + 1)].rearrange("p (d h) -> p d h", h=GH),
                            src.rearrange("p (h d) -> p d h", h=GH)).then_inc(qk_weights, 1)
                for kind, k in PREP:
                    prep_piece(0, kind, k)
                pool.wait_ge(cleared, 6)
                for g in range(NG):
                    place_v(0, g)

            def body(b, prep, post):
                first = isinstance(b, int) and b == 0
                for u in range(NG * STEPS):
                    g, s = divmod(u, STEPS)
                    if u == 1 and not first:
                        place_v(b, 2)
                    if s == 2 and g > 0 and prep:
                        place_v(b + 1, g - 1)
                    if s == 5 and not (first and g == 0):
                        normalise_o(NG * b + g - 1)
                    if prep:
                        for kind, k in PREP_AT.get(u, []):
                            prep_piece(b + 1, kind, k)
                    if post:
                        for kind, k in POST_AT.get(u, []):
                            post_piece(b - 1, kind, k)

            def tail():
                normalise_o(NG * NB - 1)
                for kind, k in POST:
                    post_piece(NB - 1, kind, k)

            batches(pool, prologue, body, tail)

        @block.scalar
        def _(act):
            def exponentials(b, g, s, h):
                n = g * TILES + s * GH + h
                act.wait_ge(scores_made, NG * TILES * b + n + 1)
                if h == 0:
                    after(act, pv_made, STEPS * NG * b + STEPS * g + s - 1)
                nc.scalar.activation(probs[:, GH * (s % 2) + h, :], scores[:, n % 3, :], ACT.Exp,
                                     scale=SCALE).then_inc(probs_made, 1)

            def take_o(slot, half):
                act.wait_ge(pv_made, STEPS * slot + 8 * half + 8)
                if half == 0:
                    after(act, o_packed, 16 * GH * slot)
                nc.scalar.copy(o_raw[:, HALF * half:HALF * (half + 1)],
                               o_acc[:, 0, :]).then_inc(o_out, 1)

            def prep_piece(b, kind, k):
                no = PREP_NO[kind, k]
                if kind == "turn":
                    act.wait_ge(prep_made, N_PREP * b + no + 1)
                    nc.scalar.copy(xt[:, k // 2, HALF * (k % 2):HALF * (k % 2 + 1)],
                                   prep_bank[0:CH, 0, :]).then_inc(prep_taken, 1)
                if kind == "qk":
                    act.wait_ge(prep_made, N_PREP * b + no + 1)
                    for g in range(NG):
                        after(act, stacked[g], 16 * 2 * len(Q_PARTS) * b)
                    cols = slice(HALF * (k % 2), HALF * (k % 2 + 1))
                    nc.scalar.copy(qk_parts[:, 0, k // 2, cols],
                                   prep_bank[:, 0, :]).then_inc(part0_done, 1)
                if kind == "v":
                    act.wait_ge(prep_made, N_PREP * b + no + 1)
                    after(act, v_ready, NG * b)
                    nc.scalar.copy(v_new[:, 2 * k:2 * k + 2, :],
                                   prep_bank[:, 0, 0:2 * C].rearrange("p (t n) -> p t n", t=2)
                                   ).then_inc(prep_taken, 1)

            def second_part(b, k):
                act.wait_ge(prep_taken, N_PREP * b + PREP_NO["qk", k] + 1)
                cols = slice(HALF * (k % 2), HALF * (k % 2 + 1))
                nc.scalar.copy(qk_parts[:, 1, k // 2, cols], rest[:, k % 2, :]).then_inc(part1_done, 1)

            def post_piece(b, kind, k):
                if kind in ("proj", "mean", "var", "mix2", "idftw"):
                    return
                act.wait_ge(post_made, N_POST * b + POST_NO[kind, k] + 1)
                two = post_bank[:, 0, 0:2 * C].rearrange("p (t n) -> p t n", t=2)
                if kind == "turn":
                    nc.scalar.copy(xt1[:, k % 2, HALF * (k // 2):HALF * (k // 2 + 1)],
                                   post_bank[0:CH, 0, :]).then_inc(post_taken, 1)
                if kind == "spread":
                    nc.scalar.copy(affine[:, :, :], two).then_inc(post_taken, 1)
                if kind in ("dftw", "idfth"):
                    nc.scalar.copy(rows_a[:, 2 * k:2 * k + 2, :], two).then_inc(post_taken, 1)
                if kind == "dfth":
                    chunk, kk = divmod(k, 3)
                    if kk < 2:
                        n = 4 - kk
                        src = post_bank[0:CH, 0, 0:P * n].rearrange("p (j r f) -> p r j f", j=n, r=2)
                        to = spec[:, chunk, :, 256 * kk:256 * kk + 64 * n].rearrange(
                            "p r (j f) -> p r j f", j=n)
                    else:
                        src = post_bank[0:CH, 0, 0:C].rearrange("p (r f) -> p r f", r=2)
                        to = spec[:, chunk, :, 448:NF]
                    nc.scalar.copy(to, src).then_inc(post_taken, 1)
                if kind == "mix1":
                    blk, half = divmod(k, 2)
                    cols = slice(NF // 2 * half, NF // 2 * (half + 1))
                    nc.scalar.activation(hidden[:, blk, cols], post_bank[0:CH, 0, 0:NF // 2], ACT.Relu,
                                         bias=mix_a_bias[:, blk:blk + 1]).then_inc(post_taken, 1)

            def prologue():
                act.wait_ge(weights_loaded, 16 * 18)
                for kind, k in PREP:
                    prep_piece(0, kind, k)
                    if kind == "qk":
                        second_part(0, k)

            def body(b, prep, post):
                first = isinstance(b, int) and b == 0
                for u in range(NG * STEPS):
                    g, s = divmod(u, STEPS)
                    slot = NG * b + g
                    jobs = [(prep_piece, b + 1, *p) for p in PREP_AT.get(u, []) if prep]
                    jobs += [(post_piece, b - 1, *p) for p in POST_AT.get(u, []) if post]
                    exponentials(b, g, s, 0)
                    exponentials(b, g, s, 1)
                    if jobs:
                        jobs[0][0](*jobs[0][1:])
                    exponentials(b, g, s, 2)
                    if s == 0 and not (first and g == 0):
                        take_o(slot - 1, 1)
                    if s == 8:
                        take_o(slot, 0)
                    exponentials(b, g, s, 3)
                    for job in jobs[1:]:
                        job[0](*job[1:])
                    if prep:
                        for kind, k in PREP_AT.get(u, []):
                            if kind == "qk":
                                second_part(b + 1, k)

            def tail():
                take_o(NG * NB - 1, 1)
                for kind, k in POST:
                    post_piece(NB - 1, kind, k)

            batches(act, prologue, body, tail)

        @block.vector
        def _(dve):
            def take_max(slot, m):
                dve.wait_ge(max_made, TILES * slot + m + 1)
                if m == 0:
                    after(dve, neg_max_done, slot)
                nc.vector.tensor_reduce(row_max[:, m:m + 1], max_tiles[:, m % 2, :], AX.X,
                                        ALU.max).then_inc(max_taken, 1)

            def join_max(slot):
                dve.wait_ge(max_taken, TILES * (slot + 1))
                nc.vector.tensor_reduce(neg_max[:, :],
                                        row_max[:, :].rearrange("p (n k) -> p n k", k=2),
                                        AX.X, ALU.max, negate=True).then_inc(neg_max_done, 1)

            def split_shift(slot):
                dve.wait_ge(shift_turned, slot + 1)
                after(dve, shift_in, 32 * slot)
                turned = prep_bank[0:GH * NT, 0, 0:P]
                nc.vector.tensor_copy(shift[:, 0, :], turned).then_inc(shift_split, 1)
                dve.wait_ge(shift_split, 2 * slot + 1)
                nc.vector.tensor_tensor(shift[:, 1, :], turned, shift[:, 0, :],
                                        ALU.subtract).then_inc(shift_split, 1)

            def invert_sums(slot):
                dve.wait_ge(sums_in, 64 * (slot + 1))
                after(dve, inv_in, 64 * slot)
                nc.vector.reciprocal(sums_inv[:, :], sums[:, :]).then_inc(sums_inverted, 1)

            def spread_inverse(slot):
                dve.wait_ge(inv_in, 64 * (slot + 1))
                alone(dve)
                nc.vector.stream_shuffle(inv_all[:, :], inv_all[:, :], [0] * 32).then_inc(inv_spread, 1)

            def statistics(which, b, taken, count, src):
                dve.wait_ge(taken, count)
                for c in range(2):
                    for half in range(2):
                        nc.vector.bn_stats(stats[:, which, c, half, :],
                                           src[:, c, HALF * half:HALF * (half + 1)]
                                           ).then_inc(stats_done[which], 1)
                dve.wait_ge(stats_done[which], 6 * b + 4)
                alone(dve)
                for c in range(2):
                    nc.vector.bn_aggr(mean_var[:, which, c, :],
                                      stats[:, which, c, :, :].rearrange("p a n -> p (a n)")
                                      ).then_inc(stats_done[which], 1)

            def normalise(which, b, what):
                dve.wait_ge(calc_done[which], CALCS * (b + 1))
                for c in range(2):
                    nc.vector.tensor_scalar(what[:, c, :], what[:, c, :], calc[:, which, 8, c:c + 1],
                                            calc[:, which, 9, c:c + 1], ALU.mult,
                                            ALU.subtract).then_inc(normed[which], 1)

            def prep_piece(b, kind, k):
                no = PREP_NO[kind, k]
                if kind in ("mean", "var"):
                    dve.wait_ge(prep_made, N_PREP * b + no + 1)
                    nc.vector.tensor_copy(calc[:, 0, 0 if kind == "mean" else 4, :],
                                          prep_bank[0:CH, 0, 0:2]).then_inc(prep_taken, 1)
                if kind == "qk":
                    dve.wait_ge(prep_made, N_PREP * b + no + 1)
                    dve.wait_ge(part0_done, 6 * b + k + 1)
                    after(dve, part2_done, 6 * b + k - 1)
                    cols = slice(HALF * (k % 2), HALF * (k % 2 + 1))
                    nc.vector.tensor_tensor(rest[:, k % 2, :], prep_bank[:, 0, :],
                                            qk_parts[:, 0, k // 2, cols],
                                            ALU.subtract).then_inc(prep_taken, 1)

            def prep_follow(b, kind, k):
                if (kind, k) == ("turn", 3):
                    statistics(0, b, prep_taken, N_PREP * b + PREP_NO["turn", 3] + 1, xt)
                if kind == "var":
                    normalise(0, b, xt)

            def post_piece(b, kind, k):
                if kind not in ("proj", "mean", "var", "mix2", "idftw"):
                    return
                dve.wait_ge(post_made, N_POST * b + POST_NO[kind, k] + 1)
                two = post_bank[:, 0, 0:2 * C].rearrange("p (t n) -> p t n", t=2)
                if kind == "proj":
                    dve.wait_ge(x1_loaded, 16 * (b + 1))
                    nc.vector.tensor_tensor(x1[:, 2 * k:2 * k + 2, :], two, x1[:, 2 * k:2 * k + 2, :],
                                            ALU.add).then_inc(post_taken, 1)
                if kind in ("mean", "var"):
                    nc.vector.tensor_copy(calc[:, 1, 0 if kind == "mean" else 4, :],
                                          post_bank[0:CH, 0, 0:2]).then_inc(post_taken, 1)
                if kind == "mix2":
                    n = P if k < 4 else SIDE
                    nc.vector.tensor_tensor(mixed[0:n, k, :], post_bank[0:n, 0, 0:2 * C],
                                            mix_b_bias[0:n, :], ALU.add).then_inc(post_taken, 1)
                if kind == "idftw":
                    dve.wait_ge(tokens_done, 6 * (b + 1))
                    nc.vector.tensor_tensor(tok_n[:, 2 * k:2 * k + 2, :], two,
                                            x1[:, 2 * k:2 * k + 2, :],
                                            ALU.add).then_inc(post_taken, 1)

            def post_follow(b, kind, k):
                if (kind, k) == ("turn", 3):
                    statistics(1, b, post_taken, N_POST * b + POST_NO["turn", 3] + 1, xt1)
                if kind == "var":
                    normalise(1, b, xt1)

            def prologue():
                nc.vector.memset(k_stack[KQ:KQ + 2, :, :], 1.0).then_inc(setup_taken, 1)
                dve.wait_ge(weights_loaded, 16 * 18)
                sign = const("sign", CH)
                nc.vector.tensor_scalar(mix_a[:, :, 0:BS], mix_a[:, :, 0:BS], sign, None,
                                        ALU.mult).then_inc(setup_taken, 1)
                nc.vector.tensor_scalar(mix_b_re[:, :, :], mix_b_re[:, :, :], sign, None,
                                        ALU.mult).then_inc(setup_taken, 1)
                dve.wait_ge(setup_made, 1)
                nc.vector.tensor_copy(bias_t[:, :, :],
                                      post_bank[0:CH, 0, 0:2 * C].rearrange("p (c n) -> p c n", c=2)
                                      ).then_inc(setup_taken, 1)
                dve.wait_ge(setup_made, 2)
                nc.vector.tensor_copy(mix_b_t[:, :, :],
                                      max_tiles[0:BS, 0, 0:NBLK * CH].rearrange(
                                          "p (b n) -> p b n", b=NBLK)).then_inc(setup_taken, 1)
                dve.wait_ge(setup_made, 3)
                nc.vector.tensor_copy(mix_b[:, :, 0:BS], mix_b_re[:, :, :]).then_inc(setup_taken, 1)
                nc.vector.tensor_tensor(mix_b[:, :, BS:CH],
                                        max_tiles[0:CH, 1, 0:C].rearrange("p (b n) -> p b n", b=NBLK),
                                        mix_b_w0[:, :, :], ALU.add).then_inc(setup_taken, 1)
                dve.wait_ge(setup_made, 4)
                nc.vector.tensor_copy(mix_b_bias[:, :], post_bank[:, 0, 0:2 * C]).then_inc(setup_taken, 1)
                for kind, k in PREP:
                    prep_piece(0, kind, k)
                    prep_follow(0, kind, k)
                for m in range(TILES):
                    take_max(0, m)
                join_max(0)
                split_shift(0)

            def body(b, prep, post):
                first = isinstance(b, int) and b == 0
                for u in range(NG * STEPS):
                    g, s = divmod(u, STEPS)
                    slot = NG * b + g
                    ahead = prep or g < NG - 1
                    jobs = [(prep_piece, b + 1, *p) for p in PREP_AT.get(u, []) if prep]
                    jobs += [(post_piece, b - 1, *p) for p in POST_AT.get(u, []) if post]
                    maxes = list(range(sum(MAX_TILES[:s]), sum(MAX_TILES[:s + 1]))) if ahead else []
                    for m in maxes[:3]:
                        take_max(slot + 1, m)
                    if s == 13 and ahead:
                        join_max(slot + 1)
                    if jobs:
                        jobs[0][0](*jobs[0][1:])
                    for m in maxes[3:]:
                        take_max(slot + 1, m)
                    if s == 14 and ahead:
                        split_shift(slot + 1)
                    for job in jobs[1:]:
                        job[0](*job[1:])
                    if prep:
                        for kind, k in PREP_AT.get(u, []):
                            prep_follow(b + 1, kind, k)
                    if post:
                        for kind, k in POST_AT.get(u, []):
                            post_follow(b - 1, kind, k)
                    if not (first and g == 0):
                        if s == 3:
                            invert_sums(slot - 1)
                        if s == 5:
                            spread_inverse(slot - 1)

            def tail():
                invert_sums(NG * NB - 1)
                spread_inverse(NG * NB - 1)
                for kind, k in POST:
                    post_piece(NB - 1, kind, k)
                    post_follow(NB - 1, kind, k)

            batches(dve, prologue, body, tail)

        @block.tensor
        def _(pe):
            mm = nc.tensor.matmul

            def score_tile(b, g, s, h):
                n = g * TILES + s * GH + h
                half, kt = divmod(s, NT)
                if s == 0 and h == 0:
                    pe.wait_ge(shift_in, 32 * (NG * b + g + 1))
                after(pe, probs_made, NG * TILES * b + n - 2)
                head = GH * g + h
                mm(scores[:, n % 3, :], k_stack[:, head, P * kt:P * (kt + 1)],
                   q_stack[:, head, HALF * half:HALF * (half + 1)],
                   start=True, stop=True).then_inc(scores_made, 1)

            def max_tile(b, g, m):
                slot = NG * b + g
                head, qt, half = GH * g + m // 16, m // 2 % NT, m % 2
                if m == 0:
                    pe.wait_ge(stacked[g], 16 * 2 * len(Q_PARTS) * (b + 1))
                after(pe, max_taken, TILES * slot + m - 1)
                mm(max_tiles[:, m % 2, :], q_stack[0:KQ, head, P * qt:P * (qt + 1)],
                   k_stack[0:KQ, head, HALF * half:HALF * (half + 1)],
                   start=True, stop=True).then_inc(max_made, 1)

            def turn_shift(slot, prep_count):
                pe.wait_ge(neg_max_done, slot + 1)
                pe.wait_ge(prep_taken, prep_count)
                nc.tensor.transpose(prep_bank[0:GH * NT, 0, 0:P], neg_max[:, :],
                                    ident).then_inc(shift_turned, 1)

            def pv(b, g, s):
                slot = NG * b + g
                half, kt = divmod(s, NT)
                pe.wait_ge(probs_made, TILES * slot + GH * (s + 1))
                if s == 0:
                    pe.wait_ge(v_ready, slot + 1)
                if kt == 0:
                    after(pe, o_out, 2 * slot + half)
                for h in range(GH):
                    last = mm(o_acc[32 * h:32 * (h + 1), 0, :], v_aug[:, g, kt, h, :],
                              probs[:, GH * (s % 2) + h, :], start=(kt == 0), stop=(kt == NT - 1),
                              skip_group_check=True)
                last.then_inc(pv_made, 1)

            def turn(bank_, src, halves, chunk):
                for n in range(4):
                    last = nc.tensor.transpose(bank_[0:CH, 0, P * n:P * (n + 1)],
                                               src[:, 4 * halves + n, CH * chunk:CH * (chunk + 1)],
                                               ident)
                return last

            def tokens_by(bank_, k, lhs, rhs):
                for n in range(2):
                    t = 2 * k + n
                    for c in range(2):
                        last = mm(bank_[:, 0, C * n:C * (n + 1)], lhs[:, c, P * t:P * (t + 1)],
                                  rhs[:, c, :], start=(c == 0), stop=(c == 1))
                return last

            def prep_piece(b, kind, k):
                no = PREP_NO[kind, k]
                after(pe, prep_taken, N_PREP * b + no)
                if no == 0:
                    pe.wait_ge(x_loaded, 16 * (b + 1))
                    after(pe, shift_split, 2 * NG * (b - 1) + 2)
                if kind == "turn":
                    last = turn(prep_bank, x_in, k % 2, k // 2)
                if kind == "mean":
                    pe.wait_ge(stats_done[0], 6 * (b + 1))
                    last = mm(prep_bank[0:CH, 0, 0:2], const("groups", CH), mean_var[:, 0, :, 0],
                              start=True, stop=True)
                if kind == "var":
                    pe.wait_ge(calc_done[0], CALCS * b + 3)
                    last = mm(prep_bank[0:CH, 0, 0:2], const("groups", CH), calc[:, 0, 3, :],
                              start=True, stop=True)
                if kind == "qk":
                    if k == 0:
                        pe.wait_ge(normed[0], 2 * (b + 1))
                    for c in range(2):
                        last = mm(prep_bank[:, 0, :], w_qk[:, c, P * (k // 2):P * (k // 2 + 1)],
                                  xt[:, c, HALF * (k % 2):HALF * (k % 2 + 1)],
                                  start=(c == 0), stop=(c == 1))
                if kind == "v":
                    last = tokens_by(prep_bank, k, xt, wv)
                last.then_inc(prep_made, 1)

            def post_piece(b, kind, k):
                no = POST_NO[kind, k]
                after(pe, post_taken, N_POST * b + no)
                if kind == "proj":
                    if k == 0:
                        pe.wait_ge(o_packed, 16 * NH * (b + 1))
                    last = tokens_by(post_bank, k, o_t, wo)
                if kind == "turn":
                    last = turn(post_bank, x1, k // 2, k % 2)
                if kind == "mean":
                    pe.wait_ge(stats_done[1], 6 * (b + 1))
                    last = mm(post_bank[0:CH, 0, 0:2], const("groups", CH), mean_var[:, 1, :, 0],
                              start=True, stop=True)
                if kind == "var":
                    pe.wait_ge(calc_done[1], CALCS * b + 3)
                    last = mm(post_bank[0:CH, 0, 0:2], const("groups", CH), calc[:, 1, 3, :],
                              start=True, stop=True)
                if kind == "spread":
                    pe.wait_ge(calc_done[1], CALCS * (b + 1))
                    for n in range(2):
                        for c in range(2):
                            last = mm(post_bank[:, 0, C * n + CH * c:C * n + CH * (c + 1)],
                                      calc[:, 1, 8 + n, c:c + 1].broadcast_to([CH, P]),
                                      cst[0:CH, where["ident"][0]:where["ident"][0] + CH],
                                      start=True, stop=True)
                if kind == "dftw":
                    pe.wait_ge(tokens_done, 6 * b + (2 if k < 2 else 4))
                    last = mm(post_bank[:, 0, 0:2 * C], const("fw"), tok_n[:, 2 * k:2 * k + 2, :],
                              start=True, stop=True)
                if kind == "dfth":
                    if k == 0:
                        pe.wait_ge(rows_in, 16 * NT * (b + 1))
                    chunk, kk = divmod(k, 3)
                    for n, j in enumerate((range(0, 4), range(4, 7), range(7, 8))[kk]):
                        f = const("fh") if j < 7 else const("fh7")
                        last = mm(post_bank[0:CH, 0, P * n:P * n + f.shape[1]],
                                  rows_b[:, j, CH * chunk:CH * (chunk + 1)], f, start=True, stop=True)
                if kind == "mix1":
                    blk, half = divmod(k, 2)
                    if k % 4 == 0:
                        pe.wait_ge(spec_in[k // 4], 64 * (b + 1))
                    last = mm(post_bank[0:CH, 0, 0:NF // 2], mix_a[:, blk, :],
                              spec_st[:, blk, NF // 2 * half:NF // 2 * (half + 1)],
                              start=True, stop=True)
                if kind == "mix2":
                    n = P if k < 4 else SIDE
                    to = post_bank[0:n, 0, 0:2 * C].rearrange("p (r b f) -> p r b f", r=2, b=NBLK)
                    for blk in range(NBLK):
                        last = mm(to[:, :, blk, :], hidden[:, blk, P * k:P * k + n], mix_b[:, blk, :],
                                  start=True, stop=True)
                if kind == "idfth":
                    if k == 0:
                        pe.wait_ge(mixed_in, 96 * (b + 1))
                    if k < 3:
                        last = mm(post_bank[:, 0, 0:2 * C], const("ih"), rows_b[:, 2 * k:2 * k + 2, :],
                                  start=True, stop=True)
                    else:
                        mm(post_bank[:, 0, 0:C], const("ih"), rows_b[:, 6, :], start=True, stop=True)
                        mm(post_bank[:, 0, C:2 * C], const("ih7a"), rows_b[:, 7, :],
                           start=True, stop=False)
                        last = mm(post_bank[:, 0, C:2 * C], const("ih7b"), rows_b[:, 8, :],
                                  start=False, stop=True)
                if kind == "idftw":
                    if k == 0:
                        pe.wait_ge(lines_in, 16 * NT * (b + 1))
                        pe.wait_ge(normed[1], 2 * (b + 1))
                    mm(post_bank[:, 0, 0:2 * C], const("iw"), rows_b[:, 2 * k:2 * k + 2, :],
                       start=True, stop=False, skip_group_check=True)
                    for n in range(2):
                        t = 2 * k + n
                        for c in range(2):
                            last = mm(post_bank[:, 0, C * n:C * (n + 1)], xt1[:, c, P * t:P * (t + 1)],
                                      bias_t[:, c, :], start=False, stop=(c == 1),
                                      skip_group_check=True)
                last.then_inc(post_made, 1)

            def setup():
                pe.wait_ge(weights_loaded, 16 * 18)
                small = cst[0:CH, where["ident"][0]:where["ident"][0] + CH]
                for c in range(2):
                    for e in range(2):
                        last = nc.tensor.transpose(post_bank[0:CH, 0, C * c + CH * e:C * c + CH * (e + 1)],
                                                   bias_rows[:, e, CH * c:CH * (c + 1)], small)
                last.then_inc(setup_made, 1)
                pe.wait_ge(setup_taken, 3)
                for blk in range(NBLK):
                    last = nc.tensor.transpose(max_tiles[0:BS, 0, CH * blk:CH * (blk + 1)],
                                               mix_b_re[:, blk, :], small)
                last.then_inc(setup_made, 1)
                pe.wait_ge(setup_taken, 5)
                for blk in range(NBLK):
                    last = mm(max_tiles[0:CH, 1, BS * blk:BS * (blk + 1)], mix_b_t[:, blk, :],
                              mix_b_w1[:, blk, :], start=True, stop=True)
                last.then_inc(setup_made, 1)
                tiny = cst[0:BS, where["ident"][0]:where["ident"][0] + BS]
                for blk in range(NBLK):
                    cols = slice(BS * blk, BS * (blk + 1))
                    real = mix_b_bias_in[:, 0, blk:blk + 1].broadcast_to([BS, P])
                    imag = mix_b_bias_in[:, 1, blk:blk + 1].broadcast_to([BS, P])
                    mm(post_bank[:, 0, BS * blk:BS * (blk + 1)], real, tiny, start=True, stop=True)
                    mm(post_bank[:, 0, C + BS * blk:C + BS * (blk + 1)], real, mix_b_w1[:, blk, :],
                       start=True, stop=False)
                    last = mm(post_bank[:, 0, C + BS * blk:C + BS * (blk + 1)], imag, tiny,
                              start=False, stop=True)
                last.then_inc(setup_made, 1)
                pe.wait_ge(setup_taken, 8)

            def prologue():
                setup()
                pe.wait_ge(qk_weights, 12)
                pe.wait_ge(cleared, 6)
                for kind, k in PREP:
                    prep_piece(0, kind, k)
                for m in range(TILES):
                    max_tile(0, 0, m)
                turn_shift(0, N_PREP)

            def body(b, prep, post):
                first = isinstance(b, int) and b == 0
                for u in range(NG * STEPS):
                    g, s = divmod(u, STEPS)
                    ahead = prep or g < NG - 1
                    nb, ng = (b, g + 1) if g < NG - 1 else (b + 1, 0)
                    jobs = [(prep_piece, b + 1, *p) for p in PREP_AT.get(u, []) if prep]
                    jobs += [(post_piece, b - 1, *p) for p in POST_AT.get(u, []) if post]
                    maxes = list(range(sum(MAX_TILES[:s]), sum(MAX_TILES[:s + 1]))) if ahead else []
                    score_tile(b, g, s, 0)
                    for m in maxes[:2]:
                        max_tile(nb, ng, m)
                    score_tile(b, g, s, 1)
                    if jobs:
                        jobs[0][0](*jobs[0][1:])
                    score_tile(b, g, s, 2)
                    for m in maxes[2:3]:
                        max_tile(nb, ng, m)
                    if s > 0:
                        pv(b, g, s - 1)
                    elif g > 0:
                        pv(b, g - 1, STEPS - 1)
                    elif not first:
                        pv(b - 1, NG - 1, STEPS - 1)
                    score_tile(b, g, s, 3)
                    for m in maxes[3:]:
                        max_tile(nb, ng, m)
                    if s == 14 and ahead:
                        turn_shift(NG * b + g + 1, N_PREP * (b + 2) if prep else N_PREP * (b + 1))
                    for job in jobs[1:]:
                        job[0](*job[1:])

            def tail():
                pv(NB - 1, NG - 1, STEPS - 1)
                for kind, k in POST:
                    post_piece(NB - 1, kind, k)

            batches(pe, prologue, body, tail)


_INS = ["x", "L0_conv_w_qkv", "L0_conv_w_o", "L1_conv_w1", "L1_conv_b1", "L1_conv_w2", "L1_conv_b2",
        "L1_conv_bias_w", "L1_conv_bias_b"]


def kernel(**inputs):
    import numpy as _np
    import concourse.bacc as _bacc
    from concourse import mybir as _mybir
    from concourse.bass_utils import run_bass_kernel_spmd as _run

    nc = _bacc.Bacc("TRN2", target_bir_lowering=False, num_devices=1)
    arrays = {"in_constants_dram": constants()[1]}
    for name in _INS:
        arrays[f"in_{name}_dram"] = _np.ascontiguousarray(inputs[name])
    args = [nc.dram_tensor(name, a.shape, _mybir.dt.from_np(a.dtype), kind="ExternalInput").ap()
            for name, a in arrays.items()]
    out = nc.dram_tensor("out_0_dram", (NB, SIDE, SIDE, C), _mybir.dt.float32,
                         kind="ExternalOutput").ap()
    build(nc, *args, out)
    r = _run(nc, [arrays], core_ids=[0])
    return r.results[0]["out_0_dram"]
```

```python
from contextlib import ExitStack

import concourse.bass as bass
import numpy as np
from concourse import mybir

ALU = mybir.AluOpType
ACT = mybir.ActivationFunctionType
AX = mybir.AxisListType
F32 = mybir.dt.float32
BF16 = mybir.dt.bfloat16

P = 128
NB, SIDE, C = 8, 32, 192
TOK = SIDE * SIDE
NT = TOK // P
CH = C // 2
NH, HD = 12, 16
GH = 4
NG = NH // GH
STEPS = 16
HALF = 512
NBLK, BS = 4, 48
NS = SIDE // 2 + 1
NF = NS * SIDE
GROUP = 6
EPS = 1e-5
SCALE = HD ** -0.5
Q_PARTS = (0, 0, 0, 1, 1, 2)
K_PARTS = (0, 1, 2, 0, 1, 0)
KQ = HD * len(Q_PARTS)
TILES = GH * STEPS
PAIRS = GH * NT
SCORE_BANKS, MAX_BANKS = 2, 3
AHEAD = STEPS + 3
STACK_INCS = 16 * 2 * len(Q_PARTS)

PREP_AT = {0: [("turn", 0), ("turn", 1)], 1: [("turn", 2), ("turn", 3)], 3: [("mean", 0)],
           4: [("var", 0)], 6: [("qk", 0)], 7: [("qk", 1)], 14: [("qk", 2)], 16: [("qk", 3)],
           18: [("qk", 4)], 19: [("qk", 5)], 20: [("v", 0)], 23: [("v", 1)], 24: [("v", 2)],
           25: [("v", 3)]}
POST_AT = {8: [("proj", 0)], 9: [("proj", 1)], 10: [("proj", 2)], 11: [("proj", 3)],
           12: [("turn", 0), ("turn", 1)], 13: [("turn", 2), ("turn", 3)],
           15: [("mean", 0)], 16: [("var", 0)], 18: [("spread", 0)],
           21: [("dftw", 0), ("dftw", 1)], 22: [("dftw", 2), ("dftw", 3)],
           26: [("dfth", 0), ("dfth", 1)], 27: [("dfth", 2), ("dfth", 3)],
           28: [("dfth", 4), ("dfth", 5)],
           30: [("mix1", 0), ("mix1", 1)], 31: [("mix1", 2), ("mix1", 3)],
           32: [("mix1", 4), ("mix1", 5)], 33: [("mix1", 6), ("mix1", 7)],
           34: [("mix2", 0)], 35: [("mix2", 1), ("mix2", 2)], 36: [("mix2", 3), ("mix2", 4)],
           39: [("idfth", 0), ("idfth", 1)], 40: [("idfth", 2), ("idfth", 3)],
           44: [("idftw", 0)], 45: [("idftw", 1)], 46: [("idftw", 2)], 47: [("idftw", 3)]}


def in_order(at):
    return [piece for step in sorted(at) for piece in at[step]]


PREP, POST = in_order(PREP_AT), in_order(POST_AT)
N_PREP, N_POST = len(PREP), len(POST)
PREP_NO = {piece: n for n, piece in enumerate(PREP)}
POST_NO = {piece: n for n, piece in enumerate(POST)}
SHIFT_AT = STEPS - 2
FIRST_AFTER_SHIFT = sum(len(p) for step, p in PREP_AT.items() if step <= SHIFT_AT)
assert max(PREP_AT) <= STEPS + SHIFT_AT
BY_TURNS = ("dftw", "dfth", "mix1", "idfth")


def on_act(kind, k):
    return kind == "spread" or kind in BY_TURNS and k % 2 == 1


TAKEN = {}
for name, order in (("prep", PREP), ("post", POST)):
    for n, piece in enumerate(order):
        TAKEN[name, piece] = sum(on_act(*p) == on_act(*piece) for p in order[:n + 1])
    for who in (True, False):
        TAKEN[name, who] = sum(on_act(*p) == who for p in order)


def w_slots():
    v_of = list(range(1, 16)) + [0, 16]
    out = {}
    for j in range(8):
        for part in range(2):
            for sl in range(2):
                out[j, part, sl] = (v_of[2 * j + sl], part == 1)
    out[7, 1, 1] = (16, False)
    return out


def constants():
    ang = 2 * np.pi / SIDE
    slots = w_slots()
    n = np.arange(SIDE)
    fw = np.zeros((P, P))
    iw = np.zeros((P, P))
    for (j, part, sl), (v, imag) in slots.items():
        weight = (1 if v in (0, 16) else 2) / SIDE
        for hl in range(4):
            row = (hl * 4 + part * 2 + sl) * 8 + j
            at = slice(hl * SIDE, (hl + 1) * SIDE)
            fw[at, row] = -np.sin(ang * v * n) if imag else np.cos(ang * v * n)
            iw[row, at] = -weight * np.sin(ang * v * n) if imag else weight * np.cos(ang * v * n)
    cos, sin = np.cos(ang * np.outer(n, n)), np.sin(ang * np.outer(n, n))
    fh = np.zeros((SIDE, 2, 2, 2, 2, SIDE))
    fh7 = np.zeros((SIDE, 2, 2, 2, 3, SIDE))
    ih = np.zeros((2, 2, SIDE, SIDE, 2, 2))
    ih7a = np.zeros((2, 2, SIDE, SIDE, 2, 2))
    ih7b = np.zeros((2, 2, SIDE, SIDE, 2, 2))
    for sl in range(2):
        fh[:, 0, sl, 0, sl] = cos
        fh[:, 1, sl, 0, sl] = sin
        fh[:, 0, sl, 1, sl] = -sin
        fh[:, 1, sl, 1, sl] = cos
        ih[0, sl, :, :, 0, sl] = cos
        ih[1, sl, :, :, 0, sl] = -sin
        ih[0, sl, :, :, 1, sl] = sin
        ih[1, sl, :, :, 1, sl] = cos
    fh7[:, :, 0, :, 0] = fh[:, :, 0, :, 0]
    for part, sl, to in ((0, 1, 1), (1, 1, 2)):
        fh7[:, part, sl, 0, to] = cos
        fh7[:, part, sl, 1, to] = -sin
    ih7a[:, 0] = ih[:, 0]
    ih7a[0, 1, :, :, 0, 1] = cos
    ih7a[1, 1, :, :, 0, 1] = -sin
    ih7b_rows = np.zeros((2, SIDE, SIDE, 2, 2))
    ih7b_rows[0, :, :, 1, 1] = cos
    ih7b_rows[1, :, :, 1, 1] = -sin
    ih7b = np.concatenate([ih7b_rows.reshape(64, P), np.zeros((64, P))])
    groups = np.zeros((P, CH))
    groups[:CH] = np.kron(np.eye(CH // GROUP), np.full((GROUP, GROUP), 1 / GROUP))
    sign = np.ones((P, 1))
    sign[BS:CH] = -1
    parts = {"ident": np.eye(P), "fw": fw, "iw": iw, "fh": fh.reshape(P, P) / SIDE,
             "fh7": fh7.reshape(P, C) / SIDE, "ih": ih.reshape(P, P), "ih7a": ih7a.reshape(P, P),
             "ih7b": ih7b, "groups": groups, "sign": sign}
    where, at = {}, 0
    for name, a in parts.items():
        where[name] = (at, a.shape[1])
        at += a.shape[1]
    return where, np.concatenate(list(parts.values()), axis=1).astype(np.float32)


def build(nc, consts, x, w_qkv, w_o, w1, b1, w2, b2, bias_w, bias_b, out):
    where, _ = constants()
    n_const = consts.shape[1]
    ctx = ExitStack()
    with ctx:
        def sb(name, shape, dt=F32):
            return ctx.enter_context(nc.sbuf_tensor(name, shape, dt))

        def bank(name, n=1):
            return ctx.enter_context(nc.psum_tensor(name, [P, n, HALF], F32))

        def sem(name):
            return ctx.enter_context(nc.semaphore(name))

        cst = sb("cst", [P, n_const])
        wv = sb("wv", [CH, 2, C])
        w_qk = sb("w_qk", [CH, 2, 2 * C])
        wo = sb("wo", [CH, 2, C])
        bias_t = sb("bias_t", [CH, 2, C])
        bias_all = sb("bias_all", [P, C])
        mix_a = sb("mix_a", [CH, NBLK, CH])
        mix_a_bias = sb("mix_a_bias", [CH, NBLK])
        mix_b = sb("mix_b", [CH, NBLK, CH])
        mix_b_bias = sb("mix_b_bias", [P, 2 * C])

        def const(name, rows=P):
            at, n = where[name]
            return cst[0:rows, at:at + n]

        ident = const("ident")

        x_in = sb("x_in", [P, NT, C])
        xt = sb("xt", [CH, 2, TOK])
        qk_parts = sb("qk_parts", [P, 3, 3, TOK], BF16)
        rest = sb("rest", [P, 2, HALF])
        q_stack = sb("q_stack", [KQ + 2, NH, TOK], BF16)
        k_stack = sb("k_stack", [KQ + 2, NH, TOK], BF16)
        v_new = sb("v_new", [P, NT, C])
        v_aug = sb("v_aug", [P, NG, NT, GH, 32])
        stats = sb("stats", [CH, 2, 2, 2, 6])
        mean_var = sb("mean_var", [CH, 2, 2, 2])
        calc = sb("calc", [CH, 2, 12, 2])
        row_max = sb("row_max", [P, 2, PAIRS])
        full_max = sb("full_max", [P, PAIRS])
        shift = sb("shift", [GH * NT, 2, P], BF16)
        probs = sb("probs", [P, 2 * GH, HALF])
        o_raw = sb("o_raw", [P, TOK])
        sums = sb("sums", [P, SIDE])
        inv_all = sb("inv_all", [P, TOK])
        o_t = sb("o_t", [CH, 2, TOK])
        x1 = sb("x1", [P, NT, C])
        xt1 = sb("xt1", [CH, 2, TOK])
        affine = sb("affine", [P, 2, C])
        tok_n = sb("tok_n", [P, NT, C])
        rows_a = sb("rows_a", [P, NT, C])
        rows_b = sb("rows_b", [P, NT + 1, C])
        spec_a = sb("spec_a", [CH, NBLK * NF])
        spec_b = sb("spec_b", [P, NBLK * NF])

        spec = spec_a[:, :].rearrange("p (c r f) -> p c r f", c=2, r=2)
        hidden = spec_a[:, :].rearrange("p (b f) -> p b f", b=NBLK)
        spec_st = spec_b[0:CH, :].rearrange("p (b f) -> p b f", b=NBLK)
        mixed = spec_b[:, 0:5 * 2 * C].rearrange("p (t n) -> p t n", t=5)

        setup_at = 0

        def setup_tile(rows, *shape):
            nonlocal setup_at
            n = int(np.prod(shape))
            flat = rows_a[:, :, :].rearrange("p t n -> p (t n)")[0:rows, setup_at:setup_at + n]
            setup_at += n
            return flat.rearrange("p (a b) -> p a b", a=shape[0])

        bias_rows = setup_tile(CH, 2, C)
        mix_b_re = setup_tile(CH, NBLK, BS)
        mix_b_t = setup_tile(BS, NBLK, CH)
        mix_b_w1 = setup_tile(BS, NBLK, BS)
        mix_b_w0 = setup_tile(CH, NBLK, BS)
        mix_b_bias_in = setup_tile(BS, 2, NBLK)
        w_raw = xt1[:, :, 0:2 * C]

        scores = bank("scores", SCORE_BANKS)
        max_tiles = bank("max_tiles", MAX_BANKS)
        o_acc = bank("o_acc")
        prep_bank = bank("prep_bank")
        post_bank = bank("post_bank")

        x_loaded = sem("x_loaded")
        x1_loaded = sem("x1_loaded")
        weights_loaded = sem("weights_loaded")
        mixer_loaded = sem("mixer_loaded")
        cleared = sem("cleared")
        stack_ones = sem("stack_ones")
        qk_weights = sem("qk_weights")
        setup_made = sem("setup_made")
        setup_taken = sem("setup_taken")
        prep_made = sem("prep_made")
        prep_taken = sem("prep_taken")
        post_made = sem("post_made")
        post_by_dve = sem("post_by_dve")
        post_by_act = sem("post_by_act")
        stats_done = [sem("prep_stats"), sem("post_stats")]
        calc_done = [sem("prep_calc"), sem("post_calc")]
        normed = [sem("prep_normed"), sem("post_normed")]
        part0_done = sem("part0_done")
        part1_done = sem("part1_done")
        part2_done = sem("part2_done")
        stacked = [sem(f"stacked{g}") for g in range(NG)]
        v_ready = sem("v_ready")
        scores_made = sem("scores_made")
        probs_made = sem("probs_made")
        pv_made = sem("pv_made")
        max_made = sem("max_made")
        max_taken = sem("max_taken")
        max_joined = sem("max_joined")
        shift_turned = sem("shift_turned")
        shift_split = sem("shift_split")
        shift_in = sem("shift_in")
        o_out = sem("o_out")
        sums_in = sem("sums_in")
        sums_inverted = sem("sums_inverted")
        inv_in = sem("inv_in")
        inv_spread = sem("inv_spread")
        o_normed = sem("o_normed")
        o_packed = sem("o_packed")
        tokens_done = sem("tokens_done")
        rows_in = sem("rows_in")
        spec_in = [sem("spec_in0"), sem("spec_in1")]
        mixed_in = sem("mixed_in")
        lines_in = sem("lines_in")
        stored = sem("stored")
        waits_alone = sem("waits_alone")

        def after(eng, s, count):
            if not isinstance(count, int) or count > 0:
                eng.wait_ge(s, count)

        def post_taken(eng, b, kind, k):
            s = post_by_act if on_act(kind, k) else post_by_dve
            after(eng, s, TAKEN["post", on_act(kind, k)] * b + TAKEN["post", (kind, k)])

        def post_sem(kind, k):
            return post_by_act if on_act(kind, k) else post_by_dve

        def alone(eng):
            eng.sem_inc(waits_alone, 1)

        def batches(eng, prologue, body, tail):
            prologue()
            body(0, True, False)
            body(1, True, True)
            with eng.Fori(2, NB - 2) as b:
                body(b, True, True)
            body(NB - 2, True, True)
            body(NB - 1, False, True)
            tail()

        def spectrum_piece(k, bank_):
            chunk, kk = divmod(k, 3)
            if kk == 2:
                return spec[:, chunk, :, 448:NF], bank_[0:CH, 0:C].rearrange("p (r f) -> p r f", r=2)
            n = 4 - kk
            src = bank_[0:CH, 0:P * n].rearrange("p (j r f) -> p r j f", j=n, r=2)
            return spec[:, chunk, :, 256 * kk:256 * kk + 64 * n].rearrange(
                "p r (j f) -> p r j f", j=n), src

        def hidden_piece(k, bank_):
            blk, half = divmod(k, 2)
            return (hidden[:, blk, NF // 2 * half:NF // 2 * (half + 1)], bank_[0:CH, 0:NF // 2],
                    mix_a_bias[:, blk:blk + 1])

        def bank_of(no, over):
            if not over:
                return post_bank[:, 0, :]
            return (post_bank[:, 0, :], prep_bank[:, 0, :], max_tiles[:, 0, :], max_tiles[:, 1, :],
                    scores[:, 0, :], scores[:, 1, :])[no % 6]

        def jobs_of(b, u, prep, post, prep_piece, post_piece):
            jobs = [(prep_piece, b + 1, *p) for p in PREP_AT.get(u, []) if prep]
            return jobs + [(post_piece, b - 1, *p, bank_of(0, False))
                           for p in POST_AT.get(u, []) if post]

        def pairs_ahead(b, u, prep):
            g, s = divmod(u + AHEAD, STEPS)
            if g >= NG and not prep:
                return []
            to = (NG * b + g, b, g) if g < NG else (NG * b + g, b + 1, g - NG)
            return [(*to, 2 * s), (*to, 2 * s + 1)]

        def image(dram, b):
            return dram[bass.ds(b, 1)].rearrange("o h w c -> (o h w) c").rearrange(
                "(t p) c -> p t c", p=P)

        CALCS = 10
        SETUP_AT = (16, 18, 20, 22, 24)
        MIXER_LOADS = 16 * 15
        block = ctx.enter_context(nc.Block())

        @block.sync
        def _(sp):
            def load_x(b):
                after(sp, prep_made, N_PREP * (b - 1) + PREP_NO["turn", 3] + 1)
                sp.dma_start(x_in[:, :, :], image(x, b)).then_inc(x_loaded, 16)

            def load_residual(b):
                if not isinstance(b, int) or b > 0:
                    post_taken(sp, b - 1, "idftw", 3)
                sp.dma_start(x1[:, :, :], image(x, b)).then_inc(x1_loaded, 16)

            def stack(b, g, which):
                to, parts = ((q_stack, Q_PARTS), (k_stack, K_PARTS))[which]
                group = NG * which + g
                after(sp, part2_done, 6 * b + 2 * (group // 2) + 2)
                alone(sp)
                after(sp, scores_made, TILES * (NG * (b - 1) + g + 1))
                for n, part in enumerate(parts):
                    sp.dma_start(to[n * HD:(n + 1) * HD, GH * g:GH * (g + 1), :],
                                 qk_parts[64 * (group % 2):64 * (group % 2 + 1), part, group // 2, :]
                                 ).then_inc(stacked[g], 16)

            def shifts(b, g):
                slot = NG * b + g
                after(sp, shift_split, 2 * slot + 2)
                for n in range(2):
                    sp.dma_start(q_stack[KQ + n:KQ + n + 1, GH * g:GH * (g + 1), :],
                                 shift[:, n, :]).then_inc(shift_in, 16)

            def sums_down(slot):
                after(sp, o_out, 2 * slot + 2)
                alone(sp)
                after(sp, inv_in, 64 * slot)
                for h in range(GH):
                    sp.dma_start(sums[32 * h:32 * (h + 1), :],
                                 o_raw[32 * h + HD:32 * h + HD + 1, :]).then_inc(sums_in, 16)

            def sums_back(slot):
                after(sp, sums_inverted, slot + 1)
                alone(sp)
                after(sp, o_normed, slot)
                for h in range(GH):
                    sp.dma_start(inv_all[32 * h:32 * h + 1, :],
                                 sums[32 * h:32 * (h + 1), :]).then_inc(inv_in, 16)

            def pack(b, g):
                after(sp, o_normed, NG * b + g + 1)
                alone(sp)
                after(sp, post_made, N_POST * (b - 1) + POST_NO["proj", 3] + 1)
                for h in range(GH):
                    head = GH * g + h
                    sp.dma_start(o_t[HD * (head % 6):HD * (head % 6 + 1), head // 6, :],
                                 o_raw[32 * h:32 * h + HD, :]).then_inc(o_packed, 16)

            def regroup_rows(b, k):
                post_taken(sp, b, "dftw", k)
                for t in (2 * k, 2 * k + 1):
                    sp.dma_start(rows_b[HD * t:HD * (t + 1), 0:NT, :],
                                 rows_a[:, t, :]).then_inc(rows_in, 16)

            def stack_spectrum(b, chunk):
                post_taken(sp, b, "dfth", 3 * chunk + 1)
                alone(sp)
                post_taken(sp, b, "dfth", 3 * chunk + 2)
                for half in range(2):
                    for part in range(2):
                        sp.dma_start(spec_st[BS * part:BS * (part + 1), 2 * chunk + half, :],
                                     spec[BS * half:BS * (half + 1), chunk, part, :]
                                     ).then_inc(spec_in[chunk], 16)

            def regroup_mixed(b):
                post_taken(sp, b, "mix2", 4)
                for part in range(2):
                    cols = slice(C * part, C * (part + 1))
                    for half in range(2):
                        sp.dma_start(rows_b[64 * part:64 * (part + 1), half:NT:2, :],
                                     mixed[64 * half:64 * (half + 1), 0:4, cols]
                                     ).then_inc(mixed_in, 16)
                    sp.dma_start(rows_b[SIDE * part:SIDE * (part + 1), NT, :],
                                 mixed[0:SIDE, 4, cols]).then_inc(mixed_in, 16)

            def regroup_lines(b):
                post_taken(sp, b, "idfth", 2)
                alone(sp)
                post_taken(sp, b, "idfth", 3)
                for t in range(NT):
                    sp.dma_start(rows_b[:, t, :],
                                 rows_a[HD * t:HD * (t + 1), 0:NT, :]).then_inc(lines_in, 16)

            def store(b):
                post_taken(sp, b, "idftw", 3)
                sp.dma_start(image(out, b), tok_n[:, :, :]).then_inc(stored, 16)

            def prologue():
                sp.dma_start(cst[:, :], consts).then_inc(weights_loaded, 16)
                sp.dma_start(x_in[:, :, :], image(x, 0)).then_inc(x_loaded, 16)
                mixer_loads = [
                    (wo[:, :, :], w_o.rearrange("(c p) n -> p c n", p=CH)),
                    (bias_rows[:, :, :], bias_w.rearrange("(c p) n -> p c n", p=CH)),
                    (bias_all[:, :], bias_b.rearrange("(o n) -> o n", o=1).partition_broadcast(P)),
                    (mix_a[0:BS, :, 0:BS], w1[0].rearrange("b d k -> d b k")),
                    (mix_a[0:BS, :, BS:CH], w1[1].rearrange("b d k -> d b k")),
                    (mix_a[BS:CH, :, 0:BS], w1[1].rearrange("b d k -> d b k")),
                    (mix_a[BS:CH, :, BS:CH], w1[0].rearrange("b d k -> d b k")),
                    (mix_b_re[0:BS, :, :], w2[0].rearrange("b d k -> d b k")),
                    (mix_b_re[BS:CH, :, :], w2[1].rearrange("b d k -> d b k")),
                    (mix_b_w1[:, :, :], w2[1].rearrange("b d k -> d b k")),
                    (mix_a_bias[0:BS, :], b1[0].rearrange("b k -> k b")),
                    (mix_a_bias[BS:CH, :], b1[1].rearrange("b k -> k b")),
                    (mix_b_bias_in[:, 0, :], b2[0].rearrange("b k -> k b")),
                    (mix_b_bias_in[:, 1, :], b2[1].rearrange("b k -> k b")),
                ]
                for c in range(2):
                    rows = slice(CH * c, CH * (c + 1))
                    sp.dma_start(w_raw[:, c, :], w_qkv[rows, 0:2 * C]).then_inc(weights_loaded, 16)
                    sp.dma_start(wv[:, c, :], w_qkv[rows, 2 * C:3 * C]).then_inc(weights_loaded, 16)
                load_x(1)
                for to, src in mixer_loads:
                    sp.dma_start(to, src, allow_slow_non_contiguous=True).then_inc(mixer_loaded, 16)
                after(sp, cleared, 1)
                sp.dma_start(mix_b_w0[BS:CH, :, :],
                             w2[0].rearrange("b d k -> d b k")).then_inc(mixer_loaded, 16)
                for g in range(NG):
                    stack(0, g, 0)
                    stack(0, g, 1)
                shifts(0, 0)

            def body(b, prep, post):
                for u in range(NG * STEPS):
                    g, s = divmod(u, STEPS)
                    slot = NG * b + g
                    first = isinstance(b, int) and b == 0
                    before = not (first and g == 0)
                    if u == 0 and post:
                        load_residual(b - 1)
                    if s == 1:
                        if before:
                            sums_down(slot - 1)
                        if g == 0 and not first:
                            stack(b, 2, 0)
                        if g > 0 and prep:
                            stack(b + 1, g - 1, 0)
                    if s == 4:
                        if before:
                            sums_back(slot - 1)
                        if g == 0 and not first:
                            stack(b, 2, 1)
                        if g > 0 and prep:
                            stack(b + 1, g - 1, 1)
                    if u == 2 and prep and (not isinstance(b, int) or b + 2 < NB):
                        load_x(b + 2)
                    if s == 7 and before:
                        if g == 0:
                            pack(b - 1, NG - 1)
                        else:
                            pack(b, g - 1)
                    if s == SHIFT_AT and (prep or g < NG - 1):
                        if g < NG - 1:
                            shifts(b, g + 1)
                        else:
                            shifts(b + 1, 0)
                    if post:
                        for kind, k in POST_AT.get(u, []):
                            if kind == "dftw":
                                regroup_rows(b - 1, k)
                            if kind == "dfth" and k % 3 == 2:
                                stack_spectrum(b - 1, k // 3)
                            if kind == "mix2" and k == 4:
                                regroup_mixed(b - 1)
                            if kind == "idfth" and k == 3:
                                regroup_lines(b - 1)
                            if kind == "idftw" and k == 3:
                                store(b - 1)

            def tail():
                b, slot = NB - 1, NG * NB - 1
                load_residual(b)
                sums_down(slot)
                sums_back(slot)
                pack(b, NG - 1)
                for k in range(4):
                    regroup_rows(b, k)
                stack_spectrum(b, 0)
                stack_spectrum(b, 1)
                regroup_mixed(b)
                regroup_lines(b)
                store(b)
                sp.wait_ge(stored, 16 * NB)

            batches(sp, prologue, body, tail)

        @block.gpsimd
        def _(pool):
            def group_value_taken(which, b, kind):
                if which == 0:
                    pool.wait_ge(prep_taken, N_PREP * b + PREP_NO[kind, 0] + 1)
                else:
                    post_taken(pool, b, kind, 0)

            def moments(which, b):
                q = calc[:, which]
                done = calc_done[which]
                mean, var = mean_var[:, which, :, 0], mean_var[:, which, :, 1]
                group_value_taken(which, b, "mean")
                nc.gpsimd.tensor_tensor(q[:, 1, :], mean, q[:, 0, :], ALU.subtract).then_inc(done, 1)
                pool.wait_ge(done, CALCS * b + 1)
                nc.gpsimd.tensor_tensor(q[:, 2, :], q[:, 1, :], q[:, 1, :], ALU.mult).then_inc(done, 1)
                pool.wait_ge(done, CALCS * b + 2)
                nc.gpsimd.tensor_tensor(q[:, 3, :], q[:, 2, :], var, ALU.add).then_inc(done, 1)

            def inverse_std(which, b):
                q = calc[:, which]
                done = calc_done[which]
                group_value_taken(which, b, "var")
                alone(pool)
                nc.gpsimd.tensor_scalar(q[:, 5, :], q[:, 4, :], EPS, None, ALU.add).then_inc(done, 1)
                pool.wait_ge(done, CALCS * b + 4)
                nc.gpsimd.tensor_tensor(q[:, 6, :], q[:, 5, :], q[:, 11, :], ALU.pow).then_inc(done, 1)
                pool.wait_ge(done, CALCS * b + 5)
                nc.gpsimd.tensor_tensor(q[:, 7, :], q[:, 6, :], q[:, 6, :], ALU.mult).then_inc(done, 1)
                pool.wait_ge(done, CALCS * b + 6)
                nc.gpsimd.tensor_tensor(q[:, 7, :], q[:, 7, :], q[:, 5, :], ALU.mult).then_inc(done, 1)
                pool.wait_ge(done, CALCS * b + 7)
                alone(pool)
                nc.gpsimd.tensor_scalar(q[:, 7, :], q[:, 7, :], -0.5, 1.5, ALU.mult,
                                        ALU.add).then_inc(done, 1)
                pool.wait_ge(done, CALCS * b + 8)
                nc.gpsimd.tensor_tensor(q[:, 8, :], q[:, 6, :], q[:, 7, :], ALU.mult).then_inc(done, 1)
                pool.wait_ge(done, CALCS * b + 9)
                nc.gpsimd.tensor_tensor(q[:, 9, :], q[:, 0, :], q[:, 8, :], ALU.mult).then_inc(done, 1)

            def last_part(b, k):
                pool.wait_ge(part1_done, 6 * b + k + 1)
                cols = slice(HALF * (k % 2), HALF * (k % 2 + 1))
                nc.gpsimd.tensor_tensor(qk_parts[:, 2, k // 2, cols], rest[:, k % 2, :],
                                        qk_parts[:, 1, k // 2, cols], ALU.subtract
                                        ).then_inc(part2_done, 1)

            def normalise_o(slot):
                pool.wait_ge(inv_spread, slot + 1)
                nc.gpsimd.tensor_tensor(o_raw[:, :], o_raw[:, :], inv_all[:, :],
                                        ALU.mult).then_inc(o_normed, 1)

            def normalise_tokens(b):
                after(pool, stored, 16 * b)
                post_taken(pool, b, "spread", 0)
                for half in range(2):
                    t = slice(4 * half, 4 * half + 4)
                    nc.gpsimd.tensor_tensor(tok_n[:, t, :], x1[:, t, :],
                                            affine[:, 0:1, :].broadcast_to([P, 4, C]),
                                            ALU.mult).then_inc(tokens_done, 1)
                    pool.wait_ge(tokens_done, 6 * b + 2 * half + 1)
                    nc.gpsimd.tensor_tensor(tok_n[:, t, :], tok_n[:, t, :],
                                            affine[:, 1:2, :].broadcast_to([P, 4, C]),
                                            ALU.subtract).then_inc(tokens_done, 1)
                for half in range(2):
                    t = slice(4 * half, 4 * half + 4)
                    nc.gpsimd.tensor_tensor(x1[:, t, :], x1[:, t, :],
                                            bias_all[:, :].unsqueeze(1).broadcast_to([P, 4, C]),
                                            ALU.add).then_inc(tokens_done, 1)

            def prep_piece(b, kind, k):
                if kind == "mean":
                    moments(0, b)
                if kind == "var":
                    inverse_std(0, b)
                if kind == "qk":
                    last_part(b, k)

            def post_piece(b, kind, k):
                if kind == "mean":
                    moments(1, b)
                if kind == "var":
                    inverse_std(1, b)
                if kind == "spread":
                    normalise_tokens(b)

            def prologue():
                nc.gpsimd.memset(mix_b_w0[:, :, :], 0.0).then_inc(cleared, 1)
                nc.gpsimd.memset(calc[:, :, 11, :], -0.5).then_inc(cleared, 1)
                nc.gpsimd.memset(inv_all[:, :], 0.0).then_inc(cleared, 1)
                nc.gpsimd.memset(rows_b[:, NT, :], 0.0).then_inc(cleared, 1)
                nc.gpsimd.memset(v_aug[:, :, :, :, :], 0.0).then_inc(cleared, 1)
                pool.wait_ge(cleared, 5)
                nc.gpsimd.memset(v_aug[:, :, :, :, HD:HD + 1], 1.0).then_inc(cleared, 1)
                pool.wait_ge(weights_loaded, 16 * 5)
                for c in range(2):
                    for group in range(2 * NG):
                        src = w_raw[:, c, 64 * group:64 * (group + 1)]
                        nc.gpsimd.tensor_copy(
                            w_qk[:, c, 64 * group:64 * (group + 1)].rearrange("p (d h) -> p d h", h=GH),
                            src.rearrange("p (h d) -> p d h", h=GH)).then_inc(qk_weights, 1)
                for kind, k in PREP:
                    prep_piece(0, kind, k)

            def body(b, prep, post):
                first = isinstance(b, int) and b == 0
                for u in range(NG * STEPS):
                    g, s = divmod(u, STEPS)
                    if s == 5 and not (first and g == 0):
                        normalise_o(NG * b + g - 1)
                    if prep:
                        for kind, k in PREP_AT.get(u, []):
                            prep_piece(b + 1, kind, k)
                    if post:
                        for kind, k in POST_AT.get(u, []):
                            post_piece(b - 1, kind, k)

            def tail():
                normalise_o(NG * NB - 1)
                for kind, k in POST:
                    post_piece(NB - 1, kind, k)

            batches(pool, prologue, body, tail)

        @block.scalar
        def _(act):
            def exponentials(b, g, s, h):
                n = g * TILES + s * GH + h
                act.wait_ge(scores_made, NG * TILES * b + n + 1)
                if h == 0:
                    after(act, pv_made, STEPS * NG * b + STEPS * g + s - 1)
                nc.scalar.activation(probs[:, GH * (s % 2) + h, :], scores[:, n % SCORE_BANKS, :], ACT.Exp,
                                     scale=SCALE).then_inc(probs_made, 1)

            def take_o(slot, half):
                act.wait_ge(pv_made, STEPS * slot + 8 * half + 8)
                if half == 0:
                    after(act, o_packed, 16 * GH * slot)
                nc.scalar.copy(o_raw[:, HALF * half:HALF * (half + 1)],
                               o_acc[:, 0, :]).then_inc(o_out, 1)

            def prep_piece(b, kind, k):
                if kind == "qk":
                    act.wait_ge(prep_made, N_PREP * b + PREP_NO[kind, k] + 1)
                    for g in range(2 if k < 2 else NG):
                        after(act, stacked[g], STACK_INCS * b)
                    cols = slice(HALF * (k % 2), HALF * (k % 2 + 1))
                    nc.scalar.copy(qk_parts[:, 0, k // 2, cols],
                                   prep_bank[:, 0, :]).then_inc(part0_done, 1)

            def post_piece(b, kind, k, bank_):
                if not on_act(kind, k):
                    return
                act.wait_ge(post_made, N_POST * b + POST_NO[kind, k] + 1)
                two = bank_[:, 0:2 * C].rearrange("p (t n) -> p t n", t=2)
                done = post_by_act
                if kind == "spread":
                    nc.scalar.copy(affine[:, :, :], two).then_inc(done, 1)
                if kind in ("dftw", "idfth"):
                    nc.scalar.copy(rows_a[:, 2 * k:2 * k + 2, :], two).then_inc(done, 1)
                if kind == "dfth":
                    nc.scalar.copy(*spectrum_piece(k, bank_)).then_inc(done, 1)
                if kind == "mix1":
                    to, src, bias = hidden_piece(k, bank_)
                    nc.scalar.activation(to, src, ACT.Relu, bias=bias).then_inc(done, 1)

            def prologue():
                act.wait_ge(weights_loaded, 16 * 5)
                for kind, k in PREP:
                    prep_piece(0, kind, k)

            def body(b, prep, post):
                first = isinstance(b, int) and b == 0
                for u in range(NG * STEPS):
                    g, s = divmod(u, STEPS)
                    slot = NG * b + g
                    jobs = jobs_of(b, u, prep, post, prep_piece, post_piece)
                    if jobs:
                        jobs[0][0](*jobs[0][1:])
                    exponentials(b, g, s, 0)
                    exponentials(b, g, s, 1)
                    if s == 0 and not (first and g == 0):
                        take_o(slot - 1, 1)
                    if s == 8:
                        take_o(slot, 0)
                    for job in jobs[1:]:
                        job[0](*job[1:])
                    exponentials(b, g, s, 2)
                    exponentials(b, g, s, 3)

            def tail():
                take_o(NG * NB - 1, 1)
                for no, (kind, k) in enumerate(POST):
                    post_piece(NB - 1, kind, k, bank_of(no, True))

            batches(act, prologue, body, tail)

        @block.vector
        def _(dve):
            def take_max(slot, g, pair, which):
                no = TILES * g + 2 * pair + which
                dve.wait_ge(max_made, TILES * slot + 2 * pair + which + 1)
                if pair == 0 and which == 0:
                    after(dve, max_joined, slot)
                nc.vector.tensor_reduce(row_max[:, which, pair:pair + 1], max_tiles[:, no % MAX_BANKS, :],
                                        AX.X, ALU.max).then_inc(max_taken, 1)
                if pair == PAIRS - 1 and which == 1:
                    dve.wait_ge(max_taken, TILES * (slot + 1))
                    after(dve, shift_turned, slot)
                    nc.vector.tensor_tensor(full_max[:, :], row_max[:, 0, :], row_max[:, 1, :],
                                            ALU.max).then_inc(max_joined, 1)

            def split_shift(slot):
                dve.wait_ge(shift_turned, slot + 1)
                after(dve, shift_in, 32 * slot)
                turned = prep_bank[0:GH * NT, 0, 0:P]
                nc.vector.tensor_scalar(shift[:, 0, :], turned, -1.0, None,
                                        ALU.mult).then_inc(shift_split, 1)
                dve.wait_ge(shift_split, 2 * slot + 1)
                nc.vector.scalar_tensor_tensor(out=shift[:, 1, :], in0=turned, scalar=-1.0,
                                               in1=shift[:, 0, :], op0=ALU.mult,
                                               op1=ALU.subtract).then_inc(shift_split, 1)

            def invert_sums(slot):
                dve.wait_ge(sums_in, 64 * (slot + 1))
                nc.vector.reciprocal(sums[:, :], sums[:, :]).then_inc(sums_inverted, 1)

            def spread_inverse(slot):
                dve.wait_ge(inv_in, 64 * (slot + 1))
                alone(dve)
                nc.vector.stream_shuffle(inv_all[:, :], inv_all[:, :], [0] * 32).then_inc(inv_spread, 1)

            def statistics(which, b, src):
                for c in range(2):
                    for half in range(2):
                        nc.vector.bn_stats(stats[:, which, c, half, :],
                                           src[:, c, HALF * half:HALF * (half + 1)]
                                           ).then_inc(stats_done[which], 1)
                dve.wait_ge(stats_done[which], 6 * b + 4)
                alone(dve)
                for c in range(2):
                    nc.vector.bn_aggr(mean_var[:, which, c, :],
                                      stats[:, which, c, :, :].rearrange("p a n -> p (a n)")
                                      ).then_inc(stats_done[which], 1)

            def normalise(which, b, what):
                dve.wait_ge(calc_done[which], CALCS * (b + 1))
                for c in range(2):
                    nc.vector.tensor_scalar(what[:, c, :], what[:, c, :], calc[:, which, 8, c:c + 1],
                                            calc[:, which, 9, c:c + 1], ALU.mult,
                                            ALU.subtract).then_inc(normed[which], 1)

            def prep_piece(b, kind, k):
                dve.wait_ge(prep_made, N_PREP * b + PREP_NO[kind, k] + 1)
                if kind == "turn":
                    nc.vector.tensor_copy(xt[:, k // 2, HALF * (k % 2):HALF * (k % 2 + 1)],
                                          prep_bank[0:CH, 0, :]).then_inc(prep_taken, 1)
                if kind in ("mean", "var"):
                    nc.vector.tensor_copy(calc[:, 0, 0 if kind == "mean" else 4, :],
                                          prep_bank[0:CH, 0, 0:2]).then_inc(prep_taken, 1)
                if kind == "qk":
                    dve.wait_ge(part0_done, 6 * b + k + 1)
                    after(dve, part2_done, 6 * b + k - 1)
                    cols = slice(HALF * (k % 2), HALF * (k % 2 + 1))
                    nc.vector.tensor_tensor(rest[:, k % 2, :], prep_bank[:, 0, :],
                                            qk_parts[:, 0, k // 2, cols],
                                            ALU.subtract).then_inc(prep_taken, 1)
                if kind == "v":
                    after(dve, v_ready, NG * b)
                    nc.vector.tensor_copy(v_new[:, 2 * k:2 * k + 2, :],
                                          prep_bank[:, 0, 0:2 * C].rearrange("p (t n) -> p t n", t=2)
                                          ).then_inc(prep_taken, 1)

            def second_part(b, k):
                dve.wait_ge(prep_taken, N_PREP * b + PREP_NO["qk", k] + 1)
                cols = slice(HALF * (k % 2), HALF * (k % 2 + 1))
                nc.vector.tensor_copy(qk_parts[:, 1, k // 2, cols], rest[:, k % 2, :]
                                      ).then_inc(part1_done, 1)

            def place_v(b, g):
                after(dve, prep_taken, N_PREP * b + PREP_NO["v", 3] + 1)
                after(dve, pv_made, STEPS * (NG * (b - 1) + g + 1))
                nc.vector.tensor_copy(
                    v_aug[:, g, :, :, 0:HD],
                    v_new[:, :, GH * HD * g:GH * HD * (g + 1)].rearrange("p t (h d) -> p t h d", h=GH)
                ).then_inc(v_ready, 1)

            def prep_follow(b, kind, k):
                if kind == "qk":
                    second_part(b, k)
                if (kind, k) == ("turn", 3):
                    dve.wait_ge(prep_taken, N_PREP * b + PREP_NO["turn", 3] + 1)
                    statistics(0, b, xt)
                if kind == "var":
                    normalise(0, b, xt)

            def post_piece(b, kind, k, bank_):
                if on_act(kind, k):
                    return
                dve.wait_ge(post_made, N_POST * b + POST_NO[kind, k] + 1)
                two = bank_[:, 0:2 * C].rearrange("p (t n) -> p t n", t=2)
                done = post_by_dve
                if kind == "proj":
                    dve.wait_ge(x1_loaded, 16 * (b + 1))
                    nc.vector.tensor_tensor(x1[:, 2 * k:2 * k + 2, :], two, x1[:, 2 * k:2 * k + 2, :],
                                            ALU.add).then_inc(done, 1)
                if kind == "turn":
                    nc.vector.tensor_copy(xt1[:, k % 2, HALF * (k // 2):HALF * (k // 2 + 1)],
                                          bank_[0:CH, :]).then_inc(done, 1)
                if kind in ("mean", "var"):
                    nc.vector.tensor_copy(calc[:, 1, 0 if kind == "mean" else 4, :],
                                          bank_[0:CH, 0:2]).then_inc(done, 1)
                if kind in ("dftw", "idfth"):
                    nc.vector.tensor_copy(rows_a[:, 2 * k:2 * k + 2, :], two).then_inc(done, 1)
                if kind == "dfth":
                    nc.vector.tensor_copy(*spectrum_piece(k, bank_)).then_inc(done, 1)
                if kind == "mix1":
                    to, src, bias = hidden_piece(k, bank_)
                    nc.vector.tensor_scalar(to, src, bias, 0.0, ALU.add, ALU.max).then_inc(done, 1)
                if kind == "mix2":
                    n = P if k < 4 else SIDE
                    nc.vector.tensor_tensor(mixed[0:n, k, :], bank_[0:n, 0:2 * C],
                                            mix_b_bias[0:n, :], ALU.add).then_inc(done, 1)
                if kind == "idftw":
                    dve.wait_ge(tokens_done, 6 * (b + 1))
                    nc.vector.tensor_tensor(tok_n[:, 2 * k:2 * k + 2, :], two,
                                            x1[:, 2 * k:2 * k + 2, :],
                                            ALU.add).then_inc(done, 1)

            def post_follow(b, kind, k):
                if (kind, k) == ("turn", 3):
                    post_taken(dve, b, "turn", 3)
                    statistics(1, b, xt1)
                if kind == "var":
                    normalise(1, b, xt1)

            def setup(stage):
                if stage > 0:
                    dve.wait_ge(setup_made, stage)
                if stage == 0:
                    signs()
                if stage == 1:
                    nc.vector.tensor_copy(bias_t[:, :, :],
                                          post_bank[0:CH, 0, 0:2 * C].rearrange("p (c n) -> p c n", c=2)
                                          ).then_inc(setup_taken, 1)
                if stage == 2:
                    nc.vector.tensor_copy(mix_b_t[:, :, :],
                                          post_bank[0:BS, 0, 0:NBLK * CH].rearrange(
                                              "p (b n) -> p b n", b=NBLK)).then_inc(setup_taken, 1)
                if stage == 3:
                    nc.vector.tensor_copy(mix_b[:, :, 0:BS], mix_b_re[:, :, :]).then_inc(setup_taken, 1)
                    nc.vector.tensor_tensor(mix_b[:, :, BS:CH],
                                            post_bank[0:CH, 0, 0:C].rearrange("p (b n) -> p b n", b=NBLK),
                                            mix_b_w0[:, :, :], ALU.add).then_inc(setup_taken, 1)
                if stage == 4:
                    nc.vector.tensor_copy(mix_b_bias[:, :],
                                          post_bank[:, 0, 0:2 * C]).then_inc(setup_taken, 1)

            def signs():
                dve.wait_ge(mixer_loaded, MIXER_LOADS)
                sign = const("sign", CH)
                nc.vector.tensor_scalar(mix_a[:, :, 0:BS], mix_a[:, :, 0:BS], sign, None,
                                        ALU.mult).then_inc(setup_taken, 1)
                nc.vector.tensor_scalar(mix_b_re[:, :, :], mix_b_re[:, :, :], sign, None,
                                        ALU.mult).then_inc(setup_taken, 1)

            def prologue():
                nc.vector.memset(k_stack[KQ:KQ + 2, :, :], 1.0).then_inc(stack_ones, 1)
                for kind, k in PREP:
                    prep_piece(0, kind, k)
                    prep_follow(0, kind, k)
                dve.wait_ge(cleared, 6)
                for g in range(NG):
                    place_v(0, g)
                for n in range(2 * AHEAD):
                    if n == PAIRS:
                        split_shift(0)
                    for which in range(2):
                        take_max(n // PAIRS, n // PAIRS, n % PAIRS, which)

            def body(b, prep, post):
                first = isinstance(b, int) and b == 0
                for u in range(NG * STEPS):
                    g, s = divmod(u, STEPS)
                    slot = NG * b + g
                    jobs = jobs_of(b, u, prep, post, prep_piece, post_piece)
                    pairs = pairs_ahead(b, u, prep)
                    if jobs:
                        jobs[0][0](*jobs[0][1:])
                    for pair in pairs[:1]:
                        take_max(pair[0], *pair[2:], 0)
                    for pair in pairs[:1]:
                        take_max(pair[0], *pair[2:], 1)
                    if s == 1 and g == 0 and not first:
                        place_v(b, 2)
                    if (g, s) in ((1, 11), (2, 2)) and prep:
                        place_v(b + 1, g - 1)
                    for job in jobs[1:]:
                        job[0](*job[1:])
                    for pair in pairs[1:]:
                        take_max(pair[0], *pair[2:], 0)
                    for pair in pairs[1:]:
                        take_max(pair[0], *pair[2:], 1)
                    if s == SHIFT_AT and (prep or g < NG - 1):
                        split_shift(slot + 1)
                    if first and u in SETUP_AT:
                        setup(SETUP_AT.index(u))
                    if prep:
                        for kind, k in PREP_AT.get(u, []):
                            prep_follow(b + 1, kind, k)
                    if post:
                        for kind, k in POST_AT.get(u, []):
                            post_follow(b - 1, kind, k)
                    if not (first and g == 0):
                        if s == 3:
                            invert_sums(slot - 1)
                        if s == 5:
                            spread_inverse(slot - 1)

            def tail():
                invert_sums(NG * NB - 1)
                spread_inverse(NG * NB - 1)
                for no, (kind, k) in enumerate(POST):
                    post_piece(NB - 1, kind, k, bank_of(no, True))
                    post_follow(NB - 1, kind, k)

            batches(dve, prologue, body, tail)

        @block.tensor
        def _(pe):
            mm = nc.tensor.matmul

            def score_tile(b, g, s, h):
                n = g * TILES + s * GH + h
                half, kt = divmod(s, NT)
                if s == 0 and h == 0:
                    pe.wait_ge(shift_in, 32 * (NG * b + g + 1))
                after(pe, probs_made, NG * TILES * b + n + 1 - SCORE_BANKS)
                head = GH * g + h
                mm(scores[:, n % SCORE_BANKS, :], k_stack[:, head, P * kt:P * (kt + 1)],
                   q_stack[:, head, HALF * half:HALF * (half + 1)],
                   start=True, stop=True).then_inc(scores_made, 1)

            def max_tile(slot, b, g, pair, which):
                no = TILES * g + 2 * pair + which
                head, qt = GH * g + pair // NT, pair % NT
                if pair == 0 and which == 0:
                    pe.wait_ge(stacked[g], STACK_INCS * (b + 1))
                after(pe, max_taken, TILES * slot + 2 * pair + which + 1 - MAX_BANKS)
                mm(max_tiles[:, no % MAX_BANKS, :], q_stack[0:KQ, head, P * qt:P * (qt + 1)],
                   k_stack[0:KQ, head, HALF * which:HALF * (which + 1)],
                   start=True, stop=True).then_inc(max_made, 1)

            def turn_shift(slot, prep_count):
                pe.wait_ge(max_joined, slot + 1)
                pe.wait_ge(prep_taken, prep_count)
                nc.tensor.transpose(prep_bank[0:PAIRS, 0, 0:P], full_max[:, :],
                                    ident).then_inc(shift_turned, 1)

            def pv(b, g, s):
                slot = NG * b + g
                half, kt = divmod(s, NT)
                pe.wait_ge(probs_made, TILES * slot + GH * (s + 1))
                if s == 0:
                    pe.wait_ge(v_ready, slot + 1)
                if kt == 0:
                    after(pe, o_out, 2 * slot + half)
                for h in range(GH):
                    last = mm(o_acc[32 * h:32 * (h + 1), 0, :], v_aug[:, g, kt, h, :],
                              probs[:, GH * (s % 2) + h, :], start=(kt == 0), stop=(kt == NT - 1),
                              skip_group_check=True)
                last.then_inc(pv_made, 1)

            def turn(bank_, src, halves, chunk):
                for n in range(4):
                    last = nc.tensor.transpose(bank_[0:CH, P * n:P * (n + 1)],
                                               src[:, 4 * halves + n, CH * chunk:CH * (chunk + 1)],
                                               ident)
                return last

            def tokens_by(bank_, k, lhs, rhs):
                for n in range(2):
                    t = 2 * k + n
                    for c in range(2):
                        last = mm(bank_[:, C * n:C * (n + 1)], lhs[:, c, P * t:P * (t + 1)],
                                  rhs[:, c, :], start=(c == 0), stop=(c == 1))
                return last

            def prep_piece(b, kind, k):
                no = PREP_NO[kind, k]
                after(pe, prep_taken, N_PREP * b + no)
                if no == 0:
                    pe.wait_ge(x_loaded, 16 * (b + 1))
                    after(pe, shift_split, 2 * NG * (b - 1) + 2)
                if no == FIRST_AFTER_SHIFT:
                    after(pe, shift_split, 2 * NG * (b - 1) + 4)
                if kind == "turn":
                    last = turn(prep_bank[:, 0, :], x_in, k % 2, k // 2)
                if kind == "mean":
                    pe.wait_ge(stats_done[0], 6 * (b + 1))
                    last = mm(prep_bank[0:CH, 0, 0:2], const("groups", CH), mean_var[:, 0, :, 0],
                              start=True, stop=True)
                if kind == "var":
                    pe.wait_ge(calc_done[0], CALCS * b + 3)
                    last = mm(prep_bank[0:CH, 0, 0:2], const("groups", CH), calc[:, 0, 3, :],
                              start=True, stop=True)
                if kind == "qk":
                    if k == 0:
                        pe.wait_ge(normed[0], 2 * (b + 1))
                    for c in range(2):
                        last = mm(prep_bank[:, 0, :], w_qk[:, c, P * (k // 2):P * (k // 2 + 1)],
                                  xt[:, c, HALF * (k % 2):HALF * (k % 2 + 1)],
                                  start=(c == 0), stop=(c == 1))
                if kind == "v":
                    last = tokens_by(prep_bank[:, 0, :], k, xt, wv)
                last.then_inc(prep_made, 1)

            def data_ready(b, kind, k):
                if kind == "proj" and k == 0:
                    post_taken(pe, b - 1, *POST[-1])
                    pe.wait_ge(scores_made, TILES * NG * NB)
                    pe.wait_ge(probs_made, TILES * NG * NB)
                if kind == "turn" and k % 2 == 0:
                    post_taken(pe, b, "proj", k + 1)
                if kind == "mix2" and k == 0:
                    post_taken(pe, b, "mix1", 6)
                    post_taken(pe, b, "mix1", 7)

            def post_piece(b, kind, k, bank_, over=False):
                no = POST_NO[kind, k]
                last_there = no - (6 if over else 1)
                if last_there >= 0:
                    post_taken(pe, b, *POST[last_there])
                elif not over and (not isinstance(b, int) or b > 0):
                    post_taken(pe, b - 1, *POST[-1])
                if over:
                    data_ready(b, kind, k)
                if kind == "proj":
                    if k == 0:
                        pe.wait_ge(o_packed, 16 * NH * (b + 1))
                    last = tokens_by(bank_, k, o_t, wo)
                if kind == "turn":
                    last = turn(bank_, x1, k // 2, k % 2)
                if kind == "mean":
                    pe.wait_ge(stats_done[1], 6 * (b + 1))
                    last = mm(bank_[0:CH, 0:2], const("groups", CH), mean_var[:, 1, :, 0],
                              start=True, stop=True)
                if kind == "var":
                    pe.wait_ge(calc_done[1], CALCS * b + 3)
                    last = mm(bank_[0:CH, 0:2], const("groups", CH), calc[:, 1, 3, :],
                              start=True, stop=True)
                if kind == "spread":
                    pe.wait_ge(calc_done[1], CALCS * (b + 1))
                    for n in range(2):
                        for c in range(2):
                            last = mm(bank_[:, C * n + CH * c:C * n + CH * (c + 1)],
                                      calc[:, 1, 8 + n, c:c + 1].broadcast_to([CH, P]),
                                      cst[0:CH, where["ident"][0]:where["ident"][0] + CH],
                                      start=True, stop=True)
                if kind == "dftw":
                    pe.wait_ge(tokens_done, 6 * b + (2 if k < 2 else 4))
                    last = mm(bank_[:, 0:2 * C], const("fw"), tok_n[:, 2 * k:2 * k + 2, :],
                              start=True, stop=True)
                if kind == "dfth":
                    if k == 0:
                        pe.wait_ge(rows_in, 16 * NT * (b + 1))
                    chunk, kk = divmod(k, 3)
                    for n, j in enumerate((range(0, 4), range(4, 7), range(7, 8))[kk]):
                        f = const("fh") if j < 7 else const("fh7")
                        last = mm(bank_[0:CH, P * n:P * n + f.shape[1]],
                                  rows_b[:, j, CH * chunk:CH * (chunk + 1)], f, start=True, stop=True)
                if kind == "mix1":
                    blk, half = divmod(k, 2)
                    if k % 4 == 0:
                        pe.wait_ge(spec_in[k // 4], 64 * (b + 1))
                    last = mm(bank_[0:CH, 0:NF // 2], mix_a[:, blk, :],
                              spec_st[:, blk, NF // 2 * half:NF // 2 * (half + 1)],
                              start=True, stop=True)
                if kind == "mix2":
                    n = P if k < 4 else SIDE
                    to = bank_[0:n, 0:2 * C].rearrange("p (r b f) -> p r b f", r=2, b=NBLK)
                    for blk in range(NBLK):
                        last = mm(to[:, :, blk, :], hidden[:, blk, P * k:P * k + n], mix_b[:, blk, :],
                                  start=True, stop=True)
                if kind == "idfth":
                    if k == 0:
                        pe.wait_ge(mixed_in, 96 * (b + 1))
                    if k < 3:
                        last = mm(bank_[:, 0:2 * C], const("ih"), rows_b[:, 2 * k:2 * k + 2, :],
                                  start=True, stop=True)
                    else:
                        mm(bank_[:, 0:C], const("ih"), rows_b[:, 6, :], start=True, stop=True)
                        mm(bank_[:, C:2 * C], const("ih7a"), rows_b[:, 7, :],
                           start=True, stop=False)
                        last = mm(bank_[:, C:2 * C], const("ih7b"), rows_b[:, 8, :],
                                  start=False, stop=True)
                if kind == "idftw":
                    if k == 0:
                        pe.wait_ge(lines_in, 16 * NT * (b + 1))
                        pe.wait_ge(normed[1], 2 * (b + 1))
                    mm(bank_[:, 0:2 * C], const("iw"), rows_b[:, 2 * k:2 * k + 2, :],
                       start=True, stop=False, skip_group_check=True)
                    for n in range(2):
                        t = 2 * k + n
                        for c in range(2):
                            last = mm(bank_[:, C * n:C * (n + 1)], xt1[:, c, P * t:P * (t + 1)],
                                      bias_t[:, c, :], start=False, stop=(c == 1),
                                      skip_group_check=True)
                last.then_inc(post_made, 1)

            def setup(stage):
                small = cst[0:CH, where["ident"][0]:where["ident"][0] + CH]
                tiny = cst[0:BS, where["ident"][0]:where["ident"][0] + BS]
                to = post_bank[:, 0, :]
                if stage == 0:
                    pe.wait_ge(mixer_loaded, MIXER_LOADS)
                    for c in range(2):
                        for e in range(2):
                            last = nc.tensor.transpose(to[0:CH, C * c + CH * e:C * c + CH * (e + 1)],
                                                       bias_rows[:, e, CH * c:CH * (c + 1)], small)
                if stage == 1:
                    pe.wait_ge(setup_taken, 3)
                    for blk in range(NBLK):
                        last = nc.tensor.transpose(to[0:BS, CH * blk:CH * (blk + 1)],
                                                   mix_b_re[:, blk, :], small)
                if stage == 2:
                    pe.wait_ge(setup_taken, 4)
                    for blk in range(NBLK):
                        last = mm(to[0:CH, BS * blk:BS * (blk + 1)], mix_b_t[:, blk, :],
                                  mix_b_w1[:, blk, :], start=True, stop=True)
                if stage == 3:
                    pe.wait_ge(setup_taken, 6)
                    for blk in range(NBLK):
                        real = mix_b_bias_in[:, 0, blk:blk + 1].broadcast_to([BS, P])
                        imag = mix_b_bias_in[:, 1, blk:blk + 1].broadcast_to([BS, P])
                        mm(to[:, BS * blk:BS * (blk + 1)], real, tiny, start=True, stop=True)
                        mm(to[:, C + BS * blk:C + BS * (blk + 1)], real, mix_b_w1[:, blk, :],
                           start=True, stop=False)
                        last = mm(to[:, C + BS * blk:C + BS * (blk + 1)], imag, tiny,
                                  start=False, stop=True)
                if stage == 4:
                    pe.wait_ge(setup_taken, 7)
                    return
                last.then_inc(setup_made, 1)

            def prologue():
                pe.wait_ge(weights_loaded, 16 * 5)
                pe.wait_ge(qk_weights, 12)
                pe.wait_ge(cleared, 6)
                pe.wait_ge(stack_ones, 1)
                for kind, k in PREP:
                    prep_piece(0, kind, k)
                for n in range(2 * AHEAD):
                    slot, pair = divmod(n, PAIRS)
                    for which in range(2):
                        max_tile(slot, 0, slot, pair, which)
                    if n == PAIRS - 1:
                        turn_shift(0, N_PREP)

            def body(b, prep, post):
                first = isinstance(b, int) and b == 0
                for u in range(NG * STEPS):
                    g, s = divmod(u, STEPS)
                    jobs = jobs_of(b, u, prep, post, prep_piece, post_piece)
                    pairs = pairs_ahead(b, u, prep)
                    tiles = [(*pair, which) for pair in pairs for which in range(2)]
                    if jobs:
                        jobs[0][0](*jobs[0][1:])
                    for tile in tiles[0:1]:
                        max_tile(*tile)
                    score_tile(b, g, s, 0)
                    for tile in tiles[1:2]:
                        max_tile(*tile)
                    score_tile(b, g, s, 1)
                    if s > 0:
                        pv(b, g, s - 1)
                    elif g > 0:
                        pv(b, g - 1, STEPS - 1)
                    elif not first:
                        pv(b - 1, NG - 1, STEPS - 1)
                    for job in jobs[1:]:
                        job[0](*job[1:])
                    for tile in tiles[2:3]:
                        max_tile(*tile)
                    score_tile(b, g, s, 2)
                    for tile in tiles[3:]:
                        max_tile(*tile)
                    score_tile(b, g, s, 3)
                    if s == SHIFT_AT and (prep or g < NG - 1):
                        made = sum(len(PREP_AT.get(n, [])) for n in range(u + 1)) if prep else 0
                        turn_shift(NG * b + g + 1, N_PREP * (b + 1) + made)
                    if first and u in SETUP_AT:
                        setup(SETUP_AT.index(u))

            def tail():
                pv(NB - 1, NG - 1, STEPS - 1)
                for no, (kind, k) in enumerate(POST):
                    post_piece(NB - 1, kind, k, bank_of(no, True), True)

            batches(pe, prologue, body, tail)


_INS = ["x", "L0_conv_w_qkv", "L0_conv_w_o", "L1_conv_w1", "L1_conv_b1", "L1_conv_w2", "L1_conv_b2",
        "L1_conv_bias_w", "L1_conv_bias_b"]


def kernel(**inputs):
    import numpy as _np
    import concourse.bacc as _bacc
    from concourse import mybir as _mybir
    from concourse.bass_utils import run_bass_kernel_spmd as _run

    nc = _bacc.Bacc("TRN2", target_bir_lowering=False, num_devices=1)
    arrays = {"in_constants_dram": constants()[1]}
    for name in _INS:
        arrays[f"in_{name}_dram"] = _np.ascontiguousarray(inputs[name])
    args = [nc.dram_tensor(name, a.shape, _mybir.dt.from_np(a.dtype), kind="ExternalInput").ap()
            for name, a in arrays.items()]
    out = nc.dram_tensor("out_0_dram", (NB, SIDE, SIDE, C), _mybir.dt.float32,
                         kind="ExternalOutput").ap()
    build(nc, *args, out)
    r = _run(nc, [arrays], core_ids=[0])
    return r.results[0]["out_0_dram"]
```

```python
from contextlib import ExitStack

import concourse.bass as bass
import numpy as np
from concourse import mybir

ALU = mybir.AluOpType
ACT = mybir.ActivationFunctionType
AX = mybir.AxisListType
F32 = mybir.dt.float32
BF16 = mybir.dt.bfloat16

P = 128
NB, SIDE, C = 8, 32, 192
TOK = SIDE * SIDE
NT = TOK // P
CH = C // 2
NH, HD = 12, 16
GH = 4
NG = NH // GH
STEPS = 16
HALF = 512
NBLK, BS = 4, 48
NS = SIDE // 2 + 1
NF = NS * SIDE
GROUP = 6
EPS = 1e-5
SCALE = HD ** -0.5
Q_PARTS = (0, 0, 0, 1, 1, 2)
K_PARTS = (0, 1, 2, 0, 1, 0)
KQ = HD * len(Q_PARTS)
TILES = GH * STEPS
PAIRS = GH * NT
HPAIRS = PAIRS // 2
SCORE_BANKS, MAX_BANKS = 2, 3
AHEAD = STEPS // 2 + 3
STACK_INCS, SECOND_INCS = 16 * 2 * len(Q_PARTS), 16 * len(Q_PARTS)

PREP_AT = {0: [("turn", 0)], 1: [("turn", 1)], 2: [("turn", 2)], 3: [("turn", 3)],
           8: [("mean", 0)], 9: [("var", 0)],
           16: [("qk", 0)], 18: [("qk", 1)], 19: [("qk", 2)], 20: [("qk", 3)], 25: [("qk", 4)],
           26: [("qk", 5)], 31: [("v", 0)], 39: [("v", 1)], 40: [("v", 2)], 41: [("v", 3)]}
POST_AT = {9: [("proj", 0)], 10: [("proj", 1)], 11: [("proj", 2), ("turn", 0)],
           12: [("proj", 3), ("turn", 1)], 13: [("turn", 2)], 14: [("turn", 3)],
           17: [("mean", 0)], 18: [("var", 0)], 20: [("spread", 0)],
           23: [("dftw", 0), ("dftw", 1)], 24: [("dftw", 2), ("dftw", 3)],
           28: [("dfth", 0), ("dfth", 1)], 29: [("dfth", 2), ("dfth", 3)],
           30: [("dfth", 4), ("dfth", 5)],
           32: [("mix1", 0), ("mix1", 1)], 33: [("mix1", 2), ("mix1", 3)],
           34: [("mix1", 4), ("mix1", 5)], 35: [("mix1", 6), ("mix1", 7)],
           36: [("mix2", 0)], 37: [("mix2", 1), ("mix2", 2)], 38: [("mix2", 3), ("mix2", 4)],
           42: [("idfth", 0), ("idfth", 1)], 43: [("idfth", 2), ("idfth", 3)],
           46: [("idftw", 0)], 47: [("idftw", 1)], 53: [("idftw", 2)], 54: [("idftw", 3)]}
PREP_FOLLOW = {1: [("stats", 0)], 2: [("stats", 1)], 3: [("stats", 2)],
               4: [("stats", 3)], 6: [("gather", 0)], 11: [("normalise", 0)],
               12: [("normalise", 1)]}
for step, pieces in PREP_AT.items():
    if pieces[0][0] == "qk":
        PREP_FOLLOW[step] = [("second_part", pieces[0][1])]
POST_FOLLOW = {12: [("stats", 0)], 13: [("stats", 1)], 14: [("stats", 2)],
               15: [("stats", 3), ("gather", 0)], 38: [("normalise", 0)], 39: [("normalise", 1)]}
PLACE_V_AT = {21: 2, 46: 0, 47: 1}
SPREAD_AT = (5, 6, 5)
TOKENS_AT = {20: (0, 1), 21: (2, 3), 32: (4,), 33: (5,)}


def in_order(at):
    return [piece for step in sorted(at) for piece in at[step]]


PREP, POST = in_order(PREP_AT), in_order(POST_AT)
LATE = {step - NG * STEPS: pieces for step, pieces in POST_AT.items() if step >= NG * STEPS}
N_PREP, N_POST = len(PREP), len(POST)
PREP_NO = {piece: n for n, piece in enumerate(PREP)}
POST_NO = {piece: n for n, piece in enumerate(POST)}
SHIFT_AT = range(STEPS // 2 - 3, NG * STEPS, STEPS // 2)
SHIFTS_BEFORE = [sum(at < step for at in SHIFT_AT) for step in sorted(PREP_AT) for _ in PREP_AT[step]]
ON_ACT = ("spread", "turn", "v")
BY_TURNS = ("dftw", "dfth", "mix1", "idfth")


def on_act(kind, k):
    return kind in ON_ACT or kind in BY_TURNS and k % 2 == 1


TAKEN = {}
for name, order in (("prep", PREP), ("post", POST)):
    for n, piece in enumerate(order):
        TAKEN[name, piece] = sum(on_act(*p) == on_act(*piece) for p in order[:n + 1])
    for who in (True, False):
        TAKEN[name, who] = sum(on_act(*p) == who for p in order)


def w_slots():
    v_of = list(range(1, 16)) + [0, 16]
    out = {}
    for j in range(8):
        for part in range(2):
            for sl in range(2):
                out[j, part, sl] = (v_of[2 * j + sl], part == 1)
    out[7, 1, 1] = (16, False)
    return out


def constants():
    ang = 2 * np.pi / SIDE
    slots = w_slots()
    n = np.arange(SIDE)
    fw = np.zeros((P, P))
    iw = np.zeros((P, P))
    for (j, part, sl), (v, imag) in slots.items():
        weight = (1 if v in (0, 16) else 2) / SIDE
        for hl in range(4):
            row = (hl * 4 + part * 2 + sl) * 8 + j
            at = slice(hl * SIDE, (hl + 1) * SIDE)
            fw[at, row] = -np.sin(ang * v * n) if imag else np.cos(ang * v * n)
            iw[row, at] = -weight * np.sin(ang * v * n) if imag else weight * np.cos(ang * v * n)
    cos, sin = np.cos(ang * np.outer(n, n)), np.sin(ang * np.outer(n, n))
    fh = np.zeros((SIDE, 2, 2, 2, 2, SIDE))
    fh7 = np.zeros((SIDE, 2, 2, 2, 3, SIDE))
    ih = np.zeros((2, 2, SIDE, SIDE, 2, 2))
    ih7a = np.zeros((2, 2, SIDE, SIDE, 2, 2))
    ih7b = np.zeros((2, 2, SIDE, SIDE, 2, 2))
    for sl in range(2):
        fh[:, 0, sl, 0, sl] = cos
        fh[:, 1, sl, 0, sl] = sin
        fh[:, 0, sl, 1, sl] = -sin
        fh[:, 1, sl, 1, sl] = cos
        ih[0, sl, :, :, 0, sl] = cos
        ih[1, sl, :, :, 0, sl] = -sin
        ih[0, sl, :, :, 1, sl] = sin
        ih[1, sl, :, :, 1, sl] = cos
    fh7[:, :, 0, :, 0] = fh[:, :, 0, :, 0]
    for part, sl, to in ((0, 1, 1), (1, 1, 2)):
        fh7[:, part, sl, 0, to] = cos
        fh7[:, part, sl, 1, to] = -sin
    ih7a[:, 0] = ih[:, 0]
    ih7a[0, 1, :, :, 0, 1] = cos
    ih7a[1, 1, :, :, 0, 1] = -sin
    ih7b_rows = np.zeros((2, SIDE, SIDE, 2, 2))
    ih7b_rows[0, :, :, 1, 1] = cos
    ih7b_rows[1, :, :, 1, 1] = -sin
    ih7b = np.concatenate([ih7b_rows.reshape(64, P), np.zeros((64, P))])
    groups = np.zeros((P, CH))
    groups[:CH] = np.kron(np.eye(CH // GROUP), np.full((GROUP, GROUP), 1 / GROUP))
    sign = np.ones((P, 1))
    sign[BS:CH] = -1
    parts = {"ident": np.eye(P), "fw": fw, "iw": iw, "fh": fh.reshape(P, P) / SIDE,
             "fh7": fh7.reshape(P, C) / SIDE, "ih": ih.reshape(P, P), "ih7a": ih7a.reshape(P, P),
             "ih7b": ih7b, "groups": groups, "sign": sign}
    where, at = {}, 0
    for name, a in parts.items():
        where[name] = (at, a.shape[1])
        at += a.shape[1]
    return where, np.concatenate(list(parts.values()), axis=1).astype(np.float32)


def build(nc, consts, x, w_qkv, w_o, w1, b1, w2, b2, bias_w, bias_b, out):
    where, _ = constants()
    n_const = consts.shape[1]
    ctx = ExitStack()
    with ctx:
        def sb(name, shape, dt=F32):
            return ctx.enter_context(nc.sbuf_tensor(name, shape, dt))

        def bank(name, n=1):
            return ctx.enter_context(nc.psum_tensor(name, [P, n, HALF], F32))

        def sem(name):
            return ctx.enter_context(nc.semaphore(name))

        cst = sb("cst", [P, n_const])
        wv = sb("wv", [CH, 2, C])
        w_qk = sb("w_qk", [CH, 2, 2 * C])
        wo = sb("wo", [CH, 2, C])
        bias_t = sb("bias_t", [CH, 2, C])
        bias_all = sb("bias_all", [P, C])
        mix_a = sb("mix_a", [CH, NBLK, CH])
        mix_a_bias = sb("mix_a_bias", [CH, NBLK])
        mix_b = sb("mix_b", [CH, NBLK, CH])
        mix_b_bias = sb("mix_b_bias", [P, 2 * C])

        def const(name, rows=P):
            at, n = where[name]
            return cst[0:rows, at:at + n]

        ident = const("ident")

        x_in = sb("x_in", [P, NT, C])
        xt = sb("xt", [CH, 2, TOK])
        qk_parts = sb("qk_parts", [P, 3, 3, TOK], BF16)
        rest = sb("rest", [P, 2, HALF])
        q_stack = sb("q_stack", [KQ + 2, NG, 2, GH, HALF], BF16)
        k_stack = sb("k_stack", [KQ + 2, NH, TOK], BF16)
        v_new = sb("v_new", [P, NT, C])
        v_aug = sb("v_aug", [P, NG, NT, GH, 32])
        stats = sb("stats", [CH, 2, 2, 2, 6])
        mean_var = sb("mean_var", [CH, 2, 2, 2])
        calc = sb("calc", [CH, 2, 12, 2])
        row_max = sb("row_max", [P, 2, HPAIRS])
        full_max = sb("full_max", [P, HPAIRS])
        shift = sb("shift", [HPAIRS, 2, P], BF16)
        probs = sb("probs", [P, 2 * GH, HALF])
        o_raw = sb("o_raw", [P, TOK])
        sums = sb("sums", [P, SIDE])
        inv_all = sb("inv_all", [P, TOK])
        o_t = sb("o_t", [CH, 2, TOK])
        x1 = sb("x1", [P, NT, C])
        xt1 = sb("xt1", [CH, 2, TOK])
        affine = sb("affine", [P, 2, C])
        tok_n = sb("tok_n", [P, NT, C])
        rows_a = sb("rows_a", [P, NT, C])
        rows_b = sb("rows_b", [P, NT + 1, C])
        spec_a = sb("spec_a", [CH, NBLK * NF])
        spec_b = sb("spec_b", [P, NBLK * NF])

        spec = spec_a[:, :].rearrange("p (c r f) -> p c r f", c=2, r=2)
        hidden = spec_a[:, :].rearrange("p (b f) -> p b f", b=NBLK)
        spec_st = spec_b[0:CH, :].rearrange("p (b f) -> p b f", b=NBLK)
        mixed = spec_b[:, 0:5 * 2 * C].rearrange("p (t n) -> p t n", t=5)

        setup_at = 0

        def setup_tile(rows, *shape):
            nonlocal setup_at
            n = int(np.prod(shape))
            flat = rows_a[:, :, :].rearrange("p t n -> p (t n)")[0:rows, setup_at:setup_at + n]
            setup_at += n
            return flat.rearrange("p (a b) -> p a b", a=shape[0])

        bias_rows = setup_tile(CH, 2, C)
        mix_b_re = setup_tile(CH, NBLK, BS)
        mix_b_t = setup_tile(BS, NBLK, CH)
        mix_b_w1 = setup_tile(BS, NBLK, BS)
        mix_b_w0 = setup_tile(CH, NBLK, BS)
        mix_b_bias_in = setup_tile(BS, 2, NBLK)
        w_raw = xt1[:, :, 0:2 * C]

        scores = bank("scores", SCORE_BANKS)
        max_tiles = bank("max_tiles", MAX_BANKS)
        o_acc = bank("o_acc")
        prep_bank = bank("prep_bank")
        post_bank = bank("post_bank")

        x_loaded = sem("x_loaded")
        x1_loaded = sem("x1_loaded")
        constants_loaded = sem("constants_loaded")
        weights_loaded = sem("weights_loaded")
        mixer_loaded = sem("mixer_loaded")
        cleared = sem("cleared")
        stack_ones = sem("stack_ones")
        qk_weights = sem("qk_weights")
        setup_made = sem("setup_made")
        setup_taken = sem("setup_taken")
        prep_made = sem("prep_made")
        prep_by_dve = sem("prep_by_dve")
        prep_by_act = sem("prep_by_act")
        post_made = sem("post_made")
        post_by_dve = sem("post_by_dve")
        post_by_act = sem("post_by_act")
        stats_done = [sem("prep_stats"), sem("post_stats")]
        calc_done = [sem("prep_calc"), sem("post_calc")]
        normed = [sem("prep_normed"), sem("post_normed")]
        part0_done = sem("part0_done")
        part1_done = sem("part1_done")
        part2_done = sem("part2_done")
        stacked = [sem(f"stacked{g}") for g in range(NG)]
        stacked_second = [sem(f"stacked_second{g}") for g in range(NG)]
        v_ready = sem("v_ready")
        scores_made = sem("scores_made")
        probs_made = sem("probs_made")
        pv_made = sem("pv_made")
        max_made = sem("max_made")
        max_taken = sem("max_taken")
        max_joined = sem("max_joined")
        shift_turned = sem("shift_turned")
        shift_split = sem("shift_split")
        shift_in = sem("shift_in")
        o_out = sem("o_out")
        sums_in = sem("sums_in")
        sums_inverted = sem("sums_inverted")
        inv_in = sem("inv_in")
        inv_spread = sem("inv_spread")
        o_normed = sem("o_normed")
        o_packed = sem("o_packed")
        tokens_done = sem("tokens_done")
        rows_in = sem("rows_in")
        spec_in = [sem("spec_in0"), sem("spec_in1")]
        mixed_in = sem("mixed_in")
        lines_in = sem("lines_in")
        stored = sem("stored")
        waits_alone = sem("waits_alone")

        def after(eng, s, count):
            if not isinstance(count, int) or count > 0:
                eng.wait_ge(s, count)

        def post_taken(eng, b, kind, k):
            s = post_by_act if on_act(kind, k) else post_by_dve
            after(eng, s, TAKEN["post", on_act(kind, k)] * b + TAKEN["post", (kind, k)])

        def prep_taken(eng, b, kind, k):
            s = prep_by_act if on_act(kind, k) else prep_by_dve
            after(eng, s, TAKEN["prep", on_act(kind, k)] * b + TAKEN["prep", (kind, k)])

        def alone(eng):
            eng.sem_inc(waits_alone, 1)

        def batches(eng, prologue, body, tail):
            prologue()
            body(0, True, False)
            body(1, True, True)
            with eng.Fori(2, NB - 2) as b:
                body(b, True, True)
            body(NB - 2, True, True)
            body(NB - 1, False, True)
            tail()

        def spectrum_piece(k, bank_):
            chunk, kk = divmod(k, 3)
            if kk == 2:
                return spec[:, chunk, :, 448:NF], bank_[0:CH, 0:C].rearrange("p (r f) -> p r f", r=2)
            n = 4 - kk
            src = bank_[0:CH, 0:P * n].rearrange("p (j r f) -> p r j f", j=n, r=2)
            return spec[:, chunk, :, 256 * kk:256 * kk + 64 * n].rearrange(
                "p r (j f) -> p r j f", j=n), src

        def hidden_piece(k, bank_):
            blk, half = divmod(k, 2)
            return (hidden[:, blk, NF // 2 * half:NF // 2 * (half + 1)], bank_[0:CH, 0:NF // 2],
                    mix_a_bias[:, blk:blk + 1])

        EARLY_BANKS, LATE_BANKS = 4, 6
        early_banks = (prep_bank[:, 0, :], post_bank[:, 0, :], scores[:, 0, :], scores[:, 1, :])
        late_banks = (post_bank[:, 0, :], prep_bank[:, 0, :], max_tiles[:, 0, :],
                      max_tiles[:, 1, :], scores[:, 0, :], scores[:, 1, :])

        def late_bank(kind, k):
            return late_banks[POST_NO[kind, k] % LATE_BANKS]

        def post_pieces(b, u, post):
            late = LATE if post and not (isinstance(b, int) and b < 2) else {}
            return ([(b - 2, *p) for p in late.get(u, [])]
                    + [(b - 1, *p) for p in POST_AT.get(u, []) if post])

        def jobs_of(b, u, prep, post, prep_piece, post_piece):
            jobs = [(prep_piece, b + 1, *p, prep_bank[:, 0, :]) for p in PREP_AT.get(u, []) if prep]
            return jobs + [(post_piece, *p, post_bank[:, 0, :]) for p in post_pieces(b, u, post)]

        def late_pieces(post_piece):
            for u in sorted(LATE):
                for p in LATE[u]:
                    post_piece(NB - 2, *p, post_bank[:, 0, :])

        def pairs_ahead(b, u, prep):
            g, s = divmod(u + AHEAD, STEPS)
            if g >= NG and not prep:
                return []
            to = (NG * b + g, b, g) if g < NG else (NG * b + g, b + 1, g - NG)
            return [(*to, 2 * s), (*to, 2 * s + 1)]

        def halves(b, g, half):
            return 2 * NG * b + 2 * g + half

        def next_half(b, u):
            g, half = divmod((u + 3) // (STEPS // 2), 2)
            return (b, g, half) if g < NG else (b + 1, 0, half)

        def shift_steps(prep):
            return SHIFT_AT if prep else SHIFT_AT[:-1]

        def image(dram, b):
            return dram[bass.ds(b, 1)].rearrange("o h w c -> (o h w) c").rearrange(
                "(t p) c -> p t c", p=P)

        def normalise_tokens(eng, ops, b, n):
            half = (0, 0, 1, 1, 0, 1)[n]
            t = slice(4 * half, 4 * half + 4)
            if n == 0:
                after(eng, stored, 16 * b)
                post_taken(eng, b, "spread", 0)
            if n in (0, 2):
                ops.tensor_tensor(tok_n[:, t, :], x1[:, t, :],
                                  affine[:, 0:1, :].broadcast_to([P, 4, C]),
                                  ALU.mult).then_inc(tokens_done, 1)
            if n in (1, 3):
                eng.wait_ge(tokens_done, 6 * b + n)
                ops.tensor_tensor(tok_n[:, t, :], tok_n[:, t, :],
                                  affine[:, 1:2, :].broadcast_to([P, 4, C]),
                                  ALU.subtract).then_inc(tokens_done, 1)
            if n in (4, 5):
                ops.tensor_tensor(x1[:, t, :], x1[:, t, :],
                                  bias_all[:, :].unsqueeze(1).broadcast_to([P, 4, C]),
                                  ALU.add).then_inc(tokens_done, 1)

        def normalise_o(eng, ops, slot):
            eng.wait_ge(inv_spread, slot + 1)
            ops.tensor_tensor(o_raw[:, :], o_raw[:, :], inv_all[:, :],
                              ALU.mult).then_inc(o_normed, 1)

        CALCS = 10
        MIXED_AT = 1 + max(step for step in POST_AT if POST_AT[step][0][0] == "mix2")
        STACK_AT = {9: "q0", 10: "q1", 11: "k"}
        BUSY = (2, 2, 1, 2, 2)
        BUSY_LATE = {"start": 10, ("turn", 3): 1, ("mean", 0): 1, ("var", 0): 2, ("spread", 0): 2,
                     ("dftw", 3): 3, ("dfth", 5): 2, ("mix2", 4): 6, "end": 2}
        SETUP_AT = (10, 12, 14, 21, 27)
        MIXER_LOADS = 16 * 15
        block = ctx.enter_context(nc.Block())

        @block.sync
        def _(sp):
            def load_x(b):
                after(sp, prep_made, N_PREP * (b - 1) + PREP_NO["turn", 3] + 1)
                sp.dma_start(x_in[:, :, :], image(x, b)).then_inc(x_loaded, 16)

            def load_residual(b):
                if not isinstance(b, int) or b > 0:
                    post_taken(sp, b - 1, "idftw", 3)
                sp.dma_start(x1[:, :, :], image(x, b)).then_inc(x1_loaded, 16)

            def stack(b, g, part_of):
                group = g if part_of != "k" else NG + g
                rows = slice(64 * (group % 2), 64 * (group % 2 + 1))
                last = {"q0": 1, "q1": 2, "k": 2}[part_of]
                after(sp, part2_done, 6 * b + 2 * (group // 2) + last)
                alone(sp)
                after(sp, scores_made, TILES * (NG * (b - 1) + g + 1))
                for n in range(len(Q_PARTS)):
                    to = slice(n * HD, (n + 1) * HD)
                    if part_of == "k":
                        sp.dma_start(k_stack[to, GH * g:GH * (g + 1), :],
                                     qk_parts[rows, K_PARTS[n], group // 2, :]
                                     ).then_inc(stacked[g], 16)
                    else:
                        half = int(part_of[1])
                        sp.dma_start(q_stack[to, g, half, :, :],
                                     qk_parts[rows, Q_PARTS[n], group // 2,
                                              HALF * half:HALF * (half + 1)]
                                     ).then_inc((stacked, stacked_second)[half][g], 16)

            def shifts(b, g, half):
                after(sp, shift_split, 2 * halves(b, g, half) + 2)
                for n in range(2):
                    sp.dma_start(q_stack[KQ + n:KQ + n + 1, g, half, :, :],
                                 shift[:, n, :]).then_inc(shift_in, 16)

            def sums_down(slot):
                after(sp, o_out, 2 * slot + 2)
                alone(sp)
                after(sp, inv_in, 64 * slot)
                for h in range(GH):
                    sp.dma_start(sums[32 * h:32 * (h + 1), :],
                                 o_raw[32 * h + HD:32 * h + HD + 1, :]).then_inc(sums_in, 16)

            def sums_back(slot):
                after(sp, sums_inverted, slot + 1)
                alone(sp)
                after(sp, o_normed, slot)
                for h in range(GH):
                    sp.dma_start(inv_all[32 * h:32 * h + 1, :],
                                 sums[32 * h:32 * (h + 1), :]).then_inc(inv_in, 16)

            def pack(b, g):
                after(sp, o_normed, NG * b + g + 1)
                alone(sp)
                after(sp, post_made, N_POST * (b - 1) + POST_NO["proj", 3] + 1)
                for h in range(GH):
                    head = GH * g + h
                    sp.dma_start(o_t[HD * (head % 6):HD * (head % 6 + 1), head // 6, :],
                                 o_raw[32 * h:32 * h + HD, :]).then_inc(o_packed, 16)

            def regroup_rows(b, k):
                post_taken(sp, b, "dftw", k)
                for t in (2 * k, 2 * k + 1):
                    sp.dma_start(rows_b[HD * t:HD * (t + 1), 0:NT, :],
                                 rows_a[:, t, :]).then_inc(rows_in, 16)

            def stack_spectrum(b, chunk):
                post_taken(sp, b, "dfth", 3 * chunk + 1)
                alone(sp)
                post_taken(sp, b, "dfth", 3 * chunk + 2)
                for half in range(2):
                    for part in range(2):
                        sp.dma_start(spec_st[BS * part:BS * (part + 1), 2 * chunk + half, :],
                                     spec[BS * half:BS * (half + 1), chunk, part, :]
                                     ).then_inc(spec_in[chunk], 16)

            def regroup_mixed(b):
                post_taken(sp, b, "mix2", 4)
                for part in range(2):
                    cols = slice(C * part, C * (part + 1))
                    for half in range(2):
                        sp.dma_start(rows_b[64 * part:64 * (part + 1), half:NT:2, :],
                                     mixed[64 * half:64 * (half + 1), 0:4, cols]
                                     ).then_inc(mixed_in, 16)
                    sp.dma_start(rows_b[SIDE * part:SIDE * (part + 1), NT, :],
                                 mixed[0:SIDE, 4, cols]).then_inc(mixed_in, 16)

            def regroup_lines(b):
                post_taken(sp, b, "idfth", 2)
                alone(sp)
                post_taken(sp, b, "idfth", 3)
                for t in range(NT):
                    sp.dma_start(rows_b[:, t, :],
                                 rows_a[HD * t:HD * (t + 1), 0:NT, :]).then_inc(lines_in, 16)

            def store(b):
                post_taken(sp, b, "idftw", 3)
                sp.dma_start(image(out, b), tok_n[:, :, :]).then_inc(stored, 16)

            def prologue():
                sp.dma_start(x_in[:, :, :], image(x, 0)).then_inc(x_loaded, 16)
                sp.dma_start(cst[:, :], consts).then_inc(constants_loaded, 16)
                mixer_loads = [
                    (wo[:, :, :], w_o.rearrange("(c p) n -> p c n", p=CH)),
                    (bias_rows[:, :, :], bias_w.rearrange("(c p) n -> p c n", p=CH)),
                    (bias_all[:, :], bias_b.rearrange("(o n) -> o n", o=1).partition_broadcast(P)),
                    (mix_a[0:BS, :, 0:BS], w1[0].rearrange("b d k -> d b k")),
                    (mix_a[0:BS, :, BS:CH], w1[1].rearrange("b d k -> d b k")),
                    (mix_a[BS:CH, :, 0:BS], w1[1].rearrange("b d k -> d b k")),
                    (mix_a[BS:CH, :, BS:CH], w1[0].rearrange("b d k -> d b k")),
                    (mix_b_re[0:BS, :, :], w2[0].rearrange("b d k -> d b k")),
                    (mix_b_re[BS:CH, :, :], w2[1].rearrange("b d k -> d b k")),
                    (mix_b_w1[:, :, :], w2[1].rearrange("b d k -> d b k")),
                    (mix_a_bias[0:BS, :], b1[0].rearrange("b k -> k b")),
                    (mix_a_bias[BS:CH, :], b1[1].rearrange("b k -> k b")),
                    (mix_b_bias_in[:, 0, :], b2[0].rearrange("b k -> k b")),
                    (mix_b_bias_in[:, 1, :], b2[1].rearrange("b k -> k b")),
                ]
                for c in range(2):
                    rows = slice(CH * c, CH * (c + 1))
                    sp.dma_start(w_raw[:, c, :], w_qkv[rows, 0:2 * C]).then_inc(weights_loaded, 16)
                    sp.dma_start(wv[:, c, :], w_qkv[rows, 2 * C:3 * C]).then_inc(weights_loaded, 16)
                load_x(1)
                for to, src in mixer_loads:
                    sp.dma_start(to, src, allow_slow_non_contiguous=True).then_inc(mixer_loaded, 16)
                after(sp, cleared, 1)
                sp.dma_start(mix_b_w0[BS:CH, :, :],
                             w2[0].rearrange("b d k -> d b k")).then_inc(mixer_loaded, 16)
                for g in range(NG):
                    for part_of in ("q0", "k", "q1"):
                        stack(0, g, part_of)
                    if g == 1:
                        shifts(0, 0, 0)

            def body(b, prep, post):
                for u in range(NG * STEPS):
                    g, s = divmod(u, STEPS)
                    slot = NG * b + g
                    first = isinstance(b, int) and b == 0
                    before = not (first and g == 0)
                    if s == 1:
                        if before:
                            sums_down(slot - 1)
                    if s == 3 and before:
                        sums_back(slot - 1)
                    if s in STACK_AT:
                        if g == 0 and not first:
                            stack(b, 2, STACK_AT[s])
                        if g > 0 and prep:
                            stack(b + 1, g - 1, STACK_AT[s])
                    if u == 7 and post:
                        load_residual(b - 1)
                    if u == 9 and prep and (not isinstance(b, int) or b + 2 < NB):
                        load_x(b + 2)
                    if s == 7 and before:
                        if g == 0:
                            pack(b - 1, NG - 1)
                        else:
                            pack(b, g - 1)
                    if post and u == MIXED_AT:
                        regroup_mixed(b - 1)
                    if u in shift_steps(prep):
                        shifts(*next_half(b, u))
                    for of, kind, k in post_pieces(b, u, post):
                        if kind == "dftw":
                            regroup_rows(of, k)
                        if kind == "dfth" and k % 3 == 2:
                            stack_spectrum(of, k // 3)
                        if kind == "idfth" and k == 3:
                            regroup_lines(of)
                        if kind == "idftw" and k == 3:
                            store(of)

            def tail():
                b, slot = NB - 1, NG * NB - 1
                sums_down(slot)
                store(b - 1)
                load_residual(b)
                sums_back(slot)
                pack(b, NG - 1)
                for k in range(4):
                    regroup_rows(b, k)
                stack_spectrum(b, 0)
                stack_spectrum(b, 1)
                regroup_mixed(b)
                regroup_lines(b)
                for k in range(4):
                    post_taken(sp, b, "idftw", k)
                    sp.dma_start(image(out, b)[:, 2 * k:2 * k + 2, :],
                                 tok_n[:, 2 * k:2 * k + 2, :]).then_inc(stored, 16)
                sp.wait_ge(stored, 16 * (NB - 1 + 4))

            batches(sp, prologue, body, tail)

        @block.gpsimd
        def _(pool):
            def group_value_taken(which, b, kind):
                if which == 0:
                    prep_taken(pool, b, kind, 0)
                else:
                    post_taken(pool, b, kind, 0)

            def moments(which, b):
                q = calc[:, which]
                done = calc_done[which]
                mean, var = mean_var[:, which, :, 0], mean_var[:, which, :, 1]
                group_value_taken(which, b, "mean")
                nc.gpsimd.tensor_tensor(q[:, 1, :], mean, q[:, 0, :], ALU.subtract).then_inc(done, 1)
                pool.wait_ge(done, CALCS * b + 1)
                nc.gpsimd.tensor_tensor(q[:, 2, :], q[:, 1, :], q[:, 1, :], ALU.mult).then_inc(done, 1)
                pool.wait_ge(done, CALCS * b + 2)
                nc.gpsimd.tensor_tensor(q[:, 3, :], q[:, 2, :], var, ALU.add).then_inc(done, 1)

            def inverse_std(which, b):
                q = calc[:, which]
                done = calc_done[which]
                group_value_taken(which, b, "var")
                alone(pool)
                nc.gpsimd.tensor_scalar(q[:, 5, :], q[:, 4, :], EPS, None, ALU.add).then_inc(done, 1)
                pool.wait_ge(done, CALCS * b + 4)
                nc.gpsimd.tensor_tensor(q[:, 6, :], q[:, 5, :], q[:, 11, :], ALU.pow).then_inc(done, 1)
                pool.wait_ge(done, CALCS * b + 5)
                nc.gpsimd.tensor_tensor(q[:, 7, :], q[:, 6, :], q[:, 6, :], ALU.mult).then_inc(done, 1)
                pool.wait_ge(done, CALCS * b + 6)
                nc.gpsimd.tensor_tensor(q[:, 7, :], q[:, 7, :], q[:, 5, :], ALU.mult).then_inc(done, 1)
                pool.wait_ge(done, CALCS * b + 7)
                alone(pool)
                nc.gpsimd.tensor_scalar(q[:, 7, :], q[:, 7, :], -0.5, 1.5, ALU.mult,
                                        ALU.add).then_inc(done, 1)
                pool.wait_ge(done, CALCS * b + 8)
                nc.gpsimd.tensor_tensor(q[:, 8, :], q[:, 6, :], q[:, 7, :], ALU.mult).then_inc(done, 1)
                pool.wait_ge(done, CALCS * b + 9)
                nc.gpsimd.tensor_tensor(q[:, 9, :], q[:, 0, :], q[:, 8, :], ALU.mult).then_inc(done, 1)

            def last_part(b, k):
                pool.wait_ge(part1_done, 6 * b + k + 1)
                cols = slice(HALF * (k % 2), HALF * (k % 2 + 1))
                nc.gpsimd.tensor_tensor(qk_parts[:, 2, k // 2, cols], rest[:, k % 2, :],
                                        qk_parts[:, 1, k // 2, cols], ALU.subtract
                                        ).then_inc(part2_done, 1)

            def prep_piece(b, kind, k):
                if kind == "mean":
                    moments(0, b)
                if kind == "var":
                    inverse_std(0, b)
                if kind == "qk":
                    last_part(b, k)

            def post_piece(b, kind, k):
                if kind == "mean":
                    moments(1, b)
                if kind == "var":
                    inverse_std(1, b)

            def prologue():
                nc.gpsimd.memset(mix_b_w0[:, :, :], 0.0).then_inc(cleared, 1)
                nc.gpsimd.memset(calc[:, :, 11, :], -0.5).then_inc(cleared, 1)
                nc.gpsimd.memset(inv_all[:, :], 0.0).then_inc(cleared, 1)
                nc.gpsimd.memset(rows_b[:, NT, :], 0.0).then_inc(cleared, 1)
                nc.gpsimd.memset(v_aug[:, :, :, :, :], 0.0).then_inc(cleared, 1)
                pool.wait_ge(cleared, 5)
                nc.gpsimd.memset(v_aug[:, :, :, :, HD:HD + 1], 1.0).then_inc(cleared, 1)
                pool.wait_ge(weights_loaded, 16 * 4)
                for c in range(2):
                    for group in range(2 * NG):
                        src = w_raw[:, c, 64 * group:64 * (group + 1)]
                        nc.gpsimd.tensor_copy(
                            w_qk[:, c, 64 * group:64 * (group + 1)].rearrange("p (d h) -> p d h", h=GH),
                            src.rearrange("p (h d) -> p d h", h=GH)).then_inc(qk_weights, 1)
                for kind, k in PREP:
                    prep_piece(0, kind, k)

            def body(b, prep, post):
                first = isinstance(b, int) and b == 0
                for u in range(NG * STEPS):
                    g, s = divmod(u, STEPS)
                    if prep:
                        for kind, k in PREP_AT.get(u, []):
                            prep_piece(b + 1, kind, k)
                    for of, kind, k in post_pieces(b, u, post):
                        post_piece(of, kind, k)
                    if post:
                        for n in TOKENS_AT.get(u, ()):
                            normalise_tokens(pool, nc.gpsimd, b - 1, n)
                    if s == SPREAD_AT[g] and not (first and g == 0):
                        normalise_o(pool, nc.gpsimd, NG * b + g - 1)

            def tail():
                for kind, k in POST:
                    post_piece(NB - 1, kind, k)
                pool.wait_ge(tokens_done, 6 * (NB - 1) + 4)
                for n in (4, 5):
                    normalise_tokens(pool, nc.gpsimd, NB - 1, n)

            batches(pool, prologue, body, tail)

        @block.scalar
        def _(act):
            def exponentials(b, g, s, h):
                n = g * TILES + s * GH + h
                act.wait_ge(scores_made, NG * TILES * b + n + 1)
                if h == 0:
                    after(act, pv_made, STEPS * NG * b + STEPS * g + s - 1)
                nc.scalar.activation(probs[:, GH * (s % 2) + h, :], scores[:, n % SCORE_BANKS, :], ACT.Exp,
                                     scale=SCALE).then_inc(probs_made, 1)

            def take_o(slot, half):
                act.wait_ge(pv_made, STEPS * slot + 8 * half + 8)
                if half == 0:
                    after(act, o_packed, 16 * GH * slot)
                nc.scalar.copy(o_raw[:, HALF * half:HALF * (half + 1)],
                               o_acc[:, 0, :]).then_inc(o_out, 1)

            def prep_piece(b, kind, k, bank_):
                if kind != "qk" and not on_act(kind, k):
                    return
                act.wait_ge(prep_made, N_PREP * b + PREP_NO[kind, k] + 1)
                if kind == "turn":
                    nc.scalar.copy(xt[:, k // 2, HALF * (k % 2):HALF * (k % 2 + 1)],
                                   bank_[0:CH, :]).then_inc(prep_by_act, 1)
                if kind == "v":
                    after(act, v_ready, NG * b)
                    nc.scalar.copy(v_new[:, 2 * k:2 * k + 2, :],
                                   bank_[:, 0:2 * C].rearrange("p (t n) -> p t n", t=2)
                                   ).then_inc(prep_by_act, 1)
                if kind == "qk":
                    for g in range(2 if k < 2 else NG):
                        after(act, stacked[g], STACK_INCS * b)
                        after(act, stacked_second[g], SECOND_INCS * b)
                    cols = slice(HALF * (k % 2), HALF * (k % 2 + 1))
                    nc.scalar.copy(qk_parts[:, 0, k // 2, cols], bank_).then_inc(part0_done, 1)

            def post_piece(b, kind, k, bank_):
                if not on_act(kind, k):
                    return
                act.wait_ge(post_made, N_POST * b + POST_NO[kind, k] + 1)
                two = bank_[:, 0:2 * C].rearrange("p (t n) -> p t n", t=2)
                done = post_by_act
                if kind == "turn":
                    nc.scalar.copy(xt1[:, k % 2, HALF * (k // 2):HALF * (k // 2 + 1)],
                                   bank_[0:CH, :]).then_inc(done, 1)
                if kind == "spread":
                    nc.scalar.copy(affine[:, :, :], two).then_inc(done, 1)
                if kind in ("dftw", "idfth"):
                    nc.scalar.copy(rows_a[:, 2 * k:2 * k + 2, :], two).then_inc(done, 1)
                if kind == "dfth":
                    nc.scalar.copy(*spectrum_piece(k, bank_)).then_inc(done, 1)
                if kind == "mix1":
                    to, src, bias = hidden_piece(k, bank_)
                    nc.scalar.activation(to, src, ACT.Relu, bias=bias).then_inc(done, 1)

            def prologue():
                act.wait_ge(cleared, 3)
                for head in range(NH):
                    nc.scalar.activation(k_stack[KQ:KQ + 2, head, :], inv_all[KQ:KQ + 2, :],
                                         ACT.Identity, bias=1.0).then_inc(stack_ones, 1)
                for no, (kind, k) in enumerate(PREP):
                    prep_piece(0, kind, k, early_banks[no % EARLY_BANKS])

            def body(b, prep, post):
                first = isinstance(b, int) and b == 0
                for u in range(NG * STEPS):
                    g, s = divmod(u, STEPS)
                    slot = NG * b + g
                    jobs = jobs_of(b, u, prep, post, prep_piece, post_piece)
                    if s == 9:
                        take_o(slot, 0)
                    if jobs:
                        jobs[0][0](*jobs[0][1:])
                    exponentials(b, g, s, 0)
                    exponentials(b, g, s, 1)
                    if s == 0 and not (first and g == 0):
                        take_o(slot - 1, 1)
                    for job in jobs[1:]:
                        job[0](*job[1:])
                    exponentials(b, g, s, 2)
                    exponentials(b, g, s, 3)

            def tail():
                take_o(NG * NB - 1, 1)
                late_pieces(post_piece)
                for kind, k in POST:
                    post_piece(NB - 1, kind, k, late_bank(kind, k))

            batches(act, prologue, body, tail)

        @block.vector
        def _(dve):
            def take_max(slot, g, pair, which):
                no = TILES * g + 2 * pair + which
                half, pair_of_half = divmod(pair, HPAIRS)
                dve.wait_ge(max_made, TILES * slot + 2 * pair + which + 1)
                if pair_of_half == 0 and which == 0:
                    after(dve, max_joined, 2 * slot + half)
                nc.vector.tensor_reduce(row_max[:, which, pair_of_half:pair_of_half + 1],
                                        max_tiles[:, no % MAX_BANKS, :],
                                        AX.X, ALU.max).then_inc(max_taken, 1)
                if pair_of_half == HPAIRS - 1 and which == 1:
                    dve.wait_ge(max_taken, TILES * slot + 2 * pair + 2)
                    after(dve, shift_turned, 2 * slot + half)
                    nc.vector.tensor_tensor(full_max[:, :], row_max[:, 0, :], row_max[:, 1, :],
                                            ALU.max).then_inc(max_joined, 1)

            def split_shift(b, g, half):
                dve.wait_ge(shift_turned, halves(b, g, half) + 1)
                after(dve, shift_in, 32 * halves(b, g, half))
                turned = prep_bank[0:HPAIRS, 0, 0:P]
                nc.vector.tensor_scalar(shift[:, 0, :], turned, -1.0, None,
                                        ALU.mult).then_inc(shift_split, 1)
                dve.wait_ge(shift_split, 2 * halves(b, g, half) + 1)
                nc.vector.scalar_tensor_tensor(out=shift[:, 1, :], in0=turned, scalar=-1.0,
                                               in1=shift[:, 0, :], op0=ALU.mult,
                                               op1=ALU.subtract).then_inc(shift_split, 1)

            def invert_sums(slot):
                dve.wait_ge(sums_in, 64 * (slot + 1))
                nc.vector.reciprocal(sums[:, :], sums[:, :]).then_inc(sums_inverted, 1)

            def spread_inverse(slot):
                dve.wait_ge(inv_in, 64 * (slot + 1))
                alone(dve)
                nc.vector.stream_shuffle(inv_all[:, :], inv_all[:, :], [0] * 32).then_inc(inv_spread, 1)

            def follow(which, b, kind, k):
                what = (xt, xt1)[which]
                if kind == "stats":
                    if which == 0:
                        c, half = divmod(k, 2)
                        prep_taken(dve, b, "turn", k)
                    else:
                        half, c = divmod(k, 2)
                        post_taken(dve, b, "turn", k)
                    nc.vector.bn_stats(stats[:, which, c, half, :],
                                       what[:, c, HALF * half:HALF * (half + 1)]
                                       ).then_inc(stats_done[which], 1)
                if kind == "gather":
                    dve.wait_ge(stats_done[which], 6 * b + 4)
                    alone(dve)
                    for c in range(2):
                        nc.vector.bn_aggr(mean_var[:, which, c, :],
                                          stats[:, which, c, :, :].rearrange("p a n -> p (a n)")
                                          ).then_inc(stats_done[which], 1)
                if kind == "normalise":
                    dve.wait_ge(calc_done[which], CALCS * (b + 1))
                    nc.vector.tensor_scalar(what[:, k, :], what[:, k, :], calc[:, which, 8, k:k + 1],
                                            calc[:, which, 9, k:k + 1], ALU.mult,
                                            ALU.subtract).then_inc(normed[which], 1)
                if kind == "second_part":
                    prep_taken(dve, b, "qk", k)
                    cols = slice(HALF * (k % 2), HALF * (k % 2 + 1))
                    nc.vector.tensor_copy(qk_parts[:, 1, k // 2, cols], rest[:, k % 2, :]
                                          ).then_inc(part1_done, 1)

            def prep_piece(b, kind, k, bank_):
                if on_act(kind, k):
                    return
                dve.wait_ge(prep_made, N_PREP * b + PREP_NO[kind, k] + 1)
                if kind in ("mean", "var"):
                    nc.vector.tensor_copy(calc[:, 0, 0 if kind == "mean" else 4, :],
                                          bank_[0:CH, 0:2]).then_inc(prep_by_dve, 1)
                if kind == "qk":
                    dve.wait_ge(part0_done, 6 * b + k + 1)
                    after(dve, part2_done, 6 * b + k - 1)
                    cols = slice(HALF * (k % 2), HALF * (k % 2 + 1))
                    nc.vector.tensor_tensor(rest[:, k % 2, :], bank_,
                                            qk_parts[:, 0, k // 2, cols],
                                            ALU.subtract).then_inc(prep_by_dve, 1)

            def place_v(b, g):
                prep_taken(dve, b, "v", 3)
                after(dve, pv_made, STEPS * (NG * (b - 1) + g + 1))
                nc.vector.tensor_copy(
                    v_aug[:, g, :, :, 0:HD],
                    v_new[:, :, GH * HD * g:GH * HD * (g + 1)].rearrange("p t (h d) -> p t h d", h=GH)
                ).then_inc(v_ready, 1)

            def post_piece(b, kind, k, bank_):
                if on_act(kind, k):
                    return
                dve.wait_ge(post_made, N_POST * b + POST_NO[kind, k] + 1)
                two = bank_[:, 0:2 * C].rearrange("p (t n) -> p t n", t=2)
                done = post_by_dve
                if kind == "proj":
                    dve.wait_ge(x1_loaded, 16 * (b + 1))
                    nc.vector.tensor_tensor(x1[:, 2 * k:2 * k + 2, :], two, x1[:, 2 * k:2 * k + 2, :],
                                            ALU.add).then_inc(done, 1)
                if kind in ("mean", "var"):
                    nc.vector.tensor_copy(calc[:, 1, 0 if kind == "mean" else 4, :],
                                          bank_[0:CH, 0:2]).then_inc(done, 1)
                if kind in ("dftw", "idfth"):
                    nc.vector.tensor_copy(rows_a[:, 2 * k:2 * k + 2, :], two).then_inc(done, 1)
                if kind == "dfth":
                    nc.vector.tensor_copy(*spectrum_piece(k, bank_)).then_inc(done, 1)
                if kind == "mix1":
                    to, src, bias = hidden_piece(k, bank_)
                    nc.vector.tensor_scalar(to, src, bias, 0.0, ALU.add, ALU.max).then_inc(done, 1)
                if kind == "mix2":
                    n = P if k < 4 else SIDE
                    nc.vector.tensor_tensor(mixed[0:n, k, :], bank_[0:n, 0:2 * C],
                                            mix_b_bias[0:n, :], ALU.add).then_inc(done, 1)
                if kind == "idftw":
                    dve.wait_ge(tokens_done, 6 * (b + 1))
                    nc.vector.tensor_tensor(tok_n[:, 2 * k:2 * k + 2, :], two,
                                            x1[:, 2 * k:2 * k + 2, :],
                                            ALU.add).then_inc(done, 1)

            def setup(stage):
                if stage > 0:
                    dve.wait_ge(setup_made, stage)
                if stage == 0:
                    signs()
                if stage == 1:
                    nc.vector.tensor_copy(bias_t[:, :, :],
                                          post_bank[0:CH, 0, 0:2 * C].rearrange("p (c n) -> p c n", c=2)
                                          ).then_inc(setup_taken, 1)
                if stage == 2:
                    nc.vector.tensor_copy(mix_b_t[:, :, :],
                                          post_bank[0:BS, 0, 0:NBLK * CH].rearrange(
                                              "p (b n) -> p b n", b=NBLK)).then_inc(setup_taken, 1)
                if stage == 3:
                    nc.vector.tensor_copy(mix_b[:, :, 0:BS], mix_b_re[:, :, :]).then_inc(setup_taken, 1)
                    nc.vector.tensor_tensor(mix_b[:, :, BS:CH],
                                            post_bank[0:CH, 0, 0:C].rearrange("p (b n) -> p b n", b=NBLK),
                                            mix_b_w0[:, :, :], ALU.add).then_inc(setup_taken, 1)
                if stage == 4:
                    nc.vector.tensor_copy(mix_b_bias[:, :],
                                          post_bank[:, 0, 0:2 * C]).then_inc(setup_taken, 1)

            def signs():
                dve.wait_ge(mixer_loaded, MIXER_LOADS)
                sign = const("sign", CH)
                nc.vector.tensor_scalar(mix_a[:, :, 0:BS], mix_a[:, :, 0:BS], sign, None,
                                        ALU.mult).then_inc(setup_taken, 1)
                nc.vector.tensor_scalar(mix_b_re[:, :, :], mix_b_re[:, :, :], sign, None,
                                        ALU.mult).then_inc(setup_taken, 1)

            def prologue():
                for u in range(NG * STEPS):
                    for kind, k in PREP_AT.get(u, []):
                        prep_piece(0, kind, k, early_banks[PREP_NO[kind, k] % EARLY_BANKS])
                    for kind, k in PREP_FOLLOW.get(u, []):
                        follow(0, 0, kind, k)
                dve.wait_ge(cleared, 6)
                for g in range(NG):
                    place_v(0, g)
                for n in range(2 * AHEAD):
                    if n == HPAIRS:
                        split_shift(0, 0, 0)
                    for which in range(2):
                        take_max(n // PAIRS, n // PAIRS, n % PAIRS, which)

            def body(b, prep, post):
                first = isinstance(b, int) and b == 0
                for u in range(NG * STEPS):
                    g, s = divmod(u, STEPS)
                    slot = NG * b + g
                    jobs = jobs_of(b, u, prep, post, prep_piece, post_piece)
                    pairs = pairs_ahead(b, u, prep)
                    if jobs:
                        jobs[0][0](*jobs[0][1:])
                    for pair in pairs[:1]:
                        take_max(pair[0], *pair[2:], 0)
                    for pair in pairs[:1]:
                        take_max(pair[0], *pair[2:], 1)
                    for job in jobs[1:]:
                        job[0](*job[1:])
                    for pair in pairs[1:]:
                        take_max(pair[0], *pair[2:], 0)
                    for pair in pairs[1:]:
                        take_max(pair[0], *pair[2:], 1)
                    if u in shift_steps(prep):
                        split_shift(*next_half(b, u))
                    if first and u in SETUP_AT:
                        setup(SETUP_AT.index(u))
                    if prep:
                        for kind, k in PREP_FOLLOW.get(u, []):
                            follow(0, b + 1, kind, k)
                    if post:
                        for kind, k in POST_FOLLOW.get(u, []):
                            follow(1, b - 1, kind, k)
                    if u in PLACE_V_AT:
                        of = PLACE_V_AT[u]
                        if of == 2 and not first:
                            place_v(b, of)
                        if of < 2 and prep:
                            place_v(b + 1, of)
                    if not (first and g == 0):
                        if s == 2:
                            invert_sums(slot - 1)
                        if s == SPREAD_AT[g]:
                            spread_inverse(slot - 1)

            def tail():
                late_pieces(post_piece)
                invert_sums(NG * NB - 1)
                spread_inverse(NG * NB - 1)
                normalise_o(dve, nc.vector, NG * NB - 1)
                for u in range(max(POST_AT) + 1):
                    for kind, k in POST_AT.get(u, []):
                        post_piece(NB - 1, kind, k, late_bank(kind, k))
                        if kind == "spread":
                            for n in range(4):
                                normalise_tokens(dve, nc.vector, NB - 1, n)
                    for kind, k in POST_FOLLOW.get(u, []):
                        follow(1, NB - 1, kind, k)

            batches(dve, prologue, body, tail)

        @block.tensor
        def _(pe):
            mm = nc.tensor.matmul

            def score_tile(b, g, s, h):
                n = g * TILES + s * GH + h
                half, kt = divmod(s, NT)
                if kt == 0 and h == 0:
                    pe.wait_ge(shift_in, 32 * (halves(b, g, half) + 1))
                after(pe, probs_made, NG * TILES * b + n + 1 - SCORE_BANKS)
                head = GH * g + h
                mm(scores[:, n % SCORE_BANKS, :], k_stack[:, head, P * kt:P * (kt + 1)],
                   q_stack[:, g, half, h, :],
                   start=True, stop=True).then_inc(scores_made, 1)

            def max_tile(slot, b, g, pair, which):
                no = TILES * g + 2 * pair + which
                half, m = divmod(pair, HPAIRS)
                h, qt = divmod(m, NT // 2)
                if pair == 0 and which == 0:
                    pe.wait_ge(stacked[g], STACK_INCS * (b + 1))
                if pair == HPAIRS and which == 0:
                    pe.wait_ge(stacked_second[g], SECOND_INCS * (b + 1))
                after(pe, max_taken, TILES * slot + 2 * pair + which + 1 - MAX_BANKS)
                mm(max_tiles[:, no % MAX_BANKS, :], q_stack[0:KQ, g, half, h, P * qt:P * (qt + 1)],
                   k_stack[0:KQ, GH * g + h, HALF * which:HALF * (which + 1)],
                   start=True, stop=True).then_inc(max_made, 1)

            def turn_shift(b, g, half, last_piece):
                pe.wait_ge(max_joined, halves(b, g, half) + 1)
                prep_taken(pe, *last_piece)
                nc.tensor.transpose(prep_bank[0:HPAIRS, 0, 0:P], full_max[:, :],
                                    ident).then_inc(shift_turned, 1)

            def pv(b, g, s):
                slot = NG * b + g
                half, kt = divmod(s, NT)
                pe.wait_ge(probs_made, TILES * slot + GH * (s + 1))
                if s == 0:
                    pe.wait_ge(v_ready, slot + 1)
                if kt == 0:
                    after(pe, o_out, 2 * slot + half)
                for h in range(GH):
                    last = mm(o_acc[32 * h:32 * (h + 1), 0, :], v_aug[:, g, kt, h, :],
                              probs[:, GH * (s % 2) + h, :], start=(kt == 0), stop=(kt == NT - 1),
                              skip_group_check=True)
                last.then_inc(pv_made, 1)

            def keep_busy(times, what=cst):
                for _ in range(times):
                    mm(o_acc[:, 0, :], what[:, 0:P], what[:, 0:HALF], start=True, stop=True)

            def turn(bank_, src, halves, chunk):
                for n in range(4):
                    last = nc.tensor.transpose(bank_[0:CH, P * n:P * (n + 1)],
                                               src[:, 4 * halves + n, CH * chunk:CH * (chunk + 1)],
                                               ident)
                return last

            def tokens_by(bank_, k, lhs, rhs, chunks=(0, 1)):
                for n in range(2):
                    t = 2 * k + n
                    for c in chunks:
                        last = mm(bank_[:, C * n:C * (n + 1)], lhs[:, c, P * t:P * (t + 1)],
                                  rhs[:, c, :], start=(n == 0 and c == 0), stop=(c == 1),
                                  skip_group_check=True)
                return last

            def linear_part(b, k, bank_):
                if k == 0:
                    pe.wait_ge(normed[1], 2 * (b + 1))
                for n in range(2):
                    t = 2 * k + n
                    for c in range(2):
                        mm(bank_[:, C * n:C * (n + 1)], xt1[:, c, P * t:P * (t + 1)],
                           bias_t[:, c, :], start=(n == 0 and c == 0), stop=False, skip_group_check=True)

            def inverse_part(b, k, bank_):
                if k == 0:
                    pe.wait_ge(lines_in, 16 * NT * (b + 1))
                return mm(bank_[:, 0:2 * C], const("iw"), rows_b[:, 2 * k:2 * k + 2, :],
                          start=False, stop=True, skip_group_check=True)

            def prep_piece(b, kind, k, bank_, early=False):
                no = PREP_NO[kind, k]
                last_there = no - (EARLY_BANKS if early else 1)
                if last_there >= 0:
                    prep_taken(pe, b, *PREP[last_there])
                elif not early:
                    prep_taken(pe, b - 1, *PREP[-1])
                if no == 0:
                    pe.wait_ge(x_loaded, 16 * (b + 1))
                if not early and (no == 0 or SHIFTS_BEFORE[no] > SHIFTS_BEFORE[no - 1]):
                    after(pe, shift_split, 2 * (2 * NG * (b - 1) + SHIFTS_BEFORE[no]) + 2)
                if kind == "turn":
                    last = turn(bank_, x_in, k % 2, k // 2)
                if kind == "mean":
                    pe.wait_ge(stats_done[0], 6 * (b + 1))
                    last = mm(bank_[0:CH, 0:2], const("groups", CH), mean_var[:, 0, :, 0],
                              start=True, stop=True)
                if kind == "var":
                    pe.wait_ge(calc_done[0], CALCS * b + 3)
                    last = mm(bank_[0:CH, 0:2], const("groups", CH), calc[:, 0, 3, :],
                              start=True, stop=True)
                if kind == "qk":
                    if k == 0:
                        pe.wait_ge(normed[0], 2 * (b + 1))
                    for c in range(2):
                        last = mm(bank_, w_qk[:, c, P * (k // 2):P * (k // 2 + 1)],
                                  xt[:, c, HALF * (k % 2):HALF * (k % 2 + 1)],
                                  start=(c == 0), stop=(c == 1))
                if kind == "v":
                    last = tokens_by(bank_, k, xt, wv)
                last.then_inc(prep_made, 1)

            def data_ready(b, kind, k):
                if kind == "turn" and k % 2 == 0:
                    post_taken(pe, b, "proj", k + 1)
                if kind == "mix2" and k == 0:
                    post_taken(pe, b, "mix1", 6)
                    post_taken(pe, b, "mix1", 7)

            def post_piece(b, kind, k, bank_, over=False):
                no = POST_NO[kind, k]
                last_there = no - (LATE_BANKS if over else 1)
                if last_there >= 0:
                    post_taken(pe, b, *POST[last_there])
                elif not over and (not isinstance(b, int) or b > 0):
                    post_taken(pe, b - 1, *POST[-1])
                if over:
                    data_ready(b, kind, k)
                if kind == "proj":
                    if k == 0:
                        pe.wait_ge(o_packed, 16 * NH * (b + 1))
                    last = tokens_by(bank_, k, o_t, wo)
                if kind == "turn":
                    last = turn(bank_, x1, k // 2, k % 2)
                if kind == "mean":
                    pe.wait_ge(stats_done[1], 6 * (b + 1))
                    last = mm(bank_[0:CH, 0:2], const("groups", CH), mean_var[:, 1, :, 0],
                              start=True, stop=True)
                if kind == "var":
                    pe.wait_ge(calc_done[1], CALCS * b + 3)
                    last = mm(bank_[0:CH, 0:2], const("groups", CH), calc[:, 1, 3, :],
                              start=True, stop=True)
                if kind == "spread":
                    pe.wait_ge(calc_done[1], CALCS * (b + 1))
                    for n in range(2):
                        for c in range(2):
                            last = mm(bank_[:, C * n + CH * c:C * n + CH * (c + 1)],
                                      calc[:, 1, 8 + n, c:c + 1].broadcast_to([CH, P]),
                                      cst[0:CH, where["ident"][0]:where["ident"][0] + CH],
                                      start=True, stop=True)
                if kind == "dftw":
                    pe.wait_ge(tokens_done, 6 * b + (2 if k < 2 else 4))
                    last = mm(bank_[:, 0:2 * C], const("fw"), tok_n[:, 2 * k:2 * k + 2, :],
                              start=True, stop=True)
                if kind == "dfth":
                    if k == 0:
                        pe.wait_ge(rows_in, 16 * NT * (b + 1))
                    chunk, kk = divmod(k, 3)
                    for n, j in enumerate((range(0, 4), range(4, 7), range(7, 8))[kk]):
                        f = const("fh") if j < 7 else const("fh7")
                        last = mm(bank_[0:CH, P * n:P * n + f.shape[1]],
                                  rows_b[:, j, CH * chunk:CH * (chunk + 1)], f, start=True, stop=True)
                if kind == "mix1":
                    blk, half = divmod(k, 2)
                    if k % 4 == 0:
                        pe.wait_ge(spec_in[k // 4], 64 * (b + 1))
                    last = mm(bank_[0:CH, 0:NF // 2], mix_a[:, blk, :],
                              spec_st[:, blk, NF // 2 * half:NF // 2 * (half + 1)],
                              start=True, stop=True)
                if kind == "mix2":
                    n = P if k < 4 else SIDE
                    to = bank_[0:n, 0:2 * C].rearrange("p (r b f) -> p r b f", r=2, b=NBLK)
                    for blk in range(NBLK):
                        last = mm(to[:, :, blk, :], hidden[:, blk, P * k:P * k + n], mix_b[:, blk, :],
                                  start=True, stop=True)
                if kind == "idfth":
                    if k == 0:
                        pe.wait_ge(mixed_in, 96 * (b + 1))
                    if k < 3:
                        last = mm(bank_[:, 0:2 * C], const("ih"), rows_b[:, 2 * k:2 * k + 2, :],
                                  start=True, stop=True)
                    else:
                        mm(bank_[:, 0:C], const("ih"), rows_b[:, 6, :], start=True, stop=True)
                        mm(bank_[:, C:2 * C], const("ih7a"), rows_b[:, 7, :],
                           start=True, stop=False)
                        last = mm(bank_[:, C:2 * C], const("ih7b"), rows_b[:, 8, :],
                                  start=False, stop=True)
                if kind == "idftw":
                    linear_part(b, k, bank_)
                    last = inverse_part(b, k, bank_)
                last.then_inc(post_made, 1)

            def setup(stage):
                small = cst[0:CH, where["ident"][0]:where["ident"][0] + CH]
                tiny = cst[0:BS, where["ident"][0]:where["ident"][0] + BS]
                to = post_bank[:, 0, :]
                if stage == 0:
                    pe.wait_ge(mixer_loaded, MIXER_LOADS)
                    for c in range(2):
                        for e in range(2):
                            last = nc.tensor.transpose(to[0:CH, C * c + CH * e:C * c + CH * (e + 1)],
                                                       bias_rows[:, e, CH * c:CH * (c + 1)], small)
                if stage == 1:
                    pe.wait_ge(setup_taken, 3)
                    for blk in range(NBLK):
                        last = nc.tensor.transpose(to[0:BS, CH * blk:CH * (blk + 1)],
                                                   mix_b_re[:, blk, :], small)
                if stage == 2:
                    pe.wait_ge(setup_taken, 4)
                    for blk in range(NBLK):
                        last = mm(to[0:CH, BS * blk:BS * (blk + 1)], mix_b_t[:, blk, :],
                                  mix_b_w1[:, blk, :], start=True, stop=True)
                if stage == 3:
                    pe.wait_ge(setup_taken, 6)
                    for blk in range(NBLK):
                        real = mix_b_bias_in[:, 0, blk:blk + 1].broadcast_to([BS, P])
                        imag = mix_b_bias_in[:, 1, blk:blk + 1].broadcast_to([BS, P])
                        mm(to[:, BS * blk:BS * (blk + 1)], real, tiny, start=True, stop=True)
                        mm(to[:, C + BS * blk:C + BS * (blk + 1)], real, mix_b_w1[:, blk, :],
                           start=True, stop=False)
                        last = mm(to[:, C + BS * blk:C + BS * (blk + 1)], imag, tiny,
                                  start=False, stop=True)
                if stage == 4:
                    pe.wait_ge(setup_taken, 7)
                    return
                last.then_inc(setup_made, 1)

            def prologue():
                pe.wait_ge(cleared, 3)
                keep_busy(BUSY[0], inv_all)
                pe.wait_ge(constants_loaded, 16)
                for no, (kind, k) in enumerate(PREP):
                    if (kind, k) == ("qk", 0):
                        pe.wait_ge(qk_weights, 12)
                        pe.wait_ge(weights_loaded, 16 * 4)
                    prep_piece(0, kind, k, early_banks[no % EARLY_BANKS], True)
                    if (kind, k) == ("turn", 3):
                        keep_busy(BUSY[1])
                    if kind == "mean":
                        keep_busy(BUSY[2])
                    if kind == "var":
                        keep_busy(BUSY[3])
                keep_busy(BUSY[4])
                pe.wait_ge(stack_ones, NH)
                pe.wait_ge(cleared, 6)
                for n in range(2 * AHEAD):
                    slot, pair = divmod(n, PAIRS)
                    for which in range(2):
                        max_tile(slot, 0, slot, pair, which)
                    if n == HPAIRS - 1:
                        turn_shift(0, 0, 0, (0, *PREP[-1]))

            def body(b, prep, post):
                first = isinstance(b, int) and b == 0
                for u in range(NG * STEPS):
                    g, s = divmod(u, STEPS)
                    jobs = jobs_of(b, u, prep, post, prep_piece, post_piece)
                    pairs = pairs_ahead(b, u, prep)
                    tiles = [(*pair, which) for pair in pairs for which in range(2)]
                    if jobs:
                        jobs[0][0](*jobs[0][1:])
                    for tile in tiles[0:1]:
                        max_tile(*tile)
                    score_tile(b, g, s, 0)
                    for tile in tiles[1:2]:
                        max_tile(*tile)
                    score_tile(b, g, s, 1)
                    if s > 0:
                        pv(b, g, s - 1)
                    elif g > 0:
                        pv(b, g - 1, STEPS - 1)
                    elif not first:
                        pv(b - 1, NG - 1, STEPS - 1)
                    for job in jobs[1:]:
                        job[0](*job[1:])
                    score_tile(b, g, s, 2)
                    for tile in tiles[2:3]:
                        max_tile(*tile)
                    score_tile(b, g, s, 3)
                    for tile in tiles[3:]:
                        max_tile(*tile)
                    if u in shift_steps(prep):
                        made = [p for step in PREP_AT if step <= u for p in PREP_AT[step] if prep]
                        turn_shift(*next_half(b, u), (b + 1, *made[-1]) if made else (b, *PREP[-1]))
                    if first and u - 1 in SETUP_AT:
                        setup(SETUP_AT.index(u - 1))

            def tail():
                pv(NB - 1, NG - 1, STEPS - 1)
                late_pieces(post_piece)
                b = NB - 1
                post_taken(pe, b - 1, *POST[-1])
                pe.wait_ge(shift_split, 4 * NG * NB)
                pe.wait_ge(max_taken, TILES * NG * NB)
                pe.wait_ge(probs_made, TILES * NG * NB)
                pe.wait_ge(o_out, 2 * NG * NB)
                pe.wait_ge(o_packed, 16 * (NH * b + GH * (NG - 1)))
                for k in range(4):
                    tokens_by(late_bank("proj", k), k, o_t, wo, (0,))
                keep_busy(BUSY_LATE["start"])
                pe.wait_ge(o_packed, 16 * NH * NB)
                for kind, k in POST:
                    if kind == "proj":
                        tokens_by(late_bank(kind, k), k, o_t, wo, (1,)).then_inc(post_made, 1)
                    elif kind != "idftw":
                        post_piece(b, kind, k, late_bank(kind, k), True)
                    keep_busy(BUSY_LATE.get((kind, k), 0))
                ends = [late_bank("idftw", k) for k in range(4)]
                for k in range(4):
                    post_taken(pe, b, *POST[POST_NO["idftw", k] - LATE_BANKS])
                    linear_part(b, k, ends[k])
                keep_busy(BUSY_LATE["end"])
                for k in range(4):
                    inverse_part(b, k, ends[k]).then_inc(post_made, 1)

            batches(pe, prologue, body, tail)


_INS = ["x", "L0_conv_w_qkv", "L0_conv_w_o", "L1_conv_w1", "L1_conv_b1", "L1_conv_w2", "L1_conv_b2",
        "L1_conv_bias_w", "L1_conv_bias_b"]


def kernel(**inputs):
    import numpy as _np
    import concourse.bacc as _bacc
    from concourse import mybir as _mybir
    from concourse.bass_utils import run_bass_kernel_spmd as _run

    nc = _bacc.Bacc("TRN2", target_bir_lowering=False, num_devices=1)
    arrays = {"in_constants_dram": constants()[1]}
    for name in _INS:
        arrays[f"in_{name}_dram"] = _np.ascontiguousarray(inputs[name])
    args = [nc.dram_tensor(name, a.shape, _mybir.dt.from_np(a.dtype), kind="ExternalInput").ap()
            for name, a in arrays.items()]
    out = nc.dram_tensor("out_0_dram", (NB, SIDE, SIDE, C), _mybir.dt.float32,
                         kind="ExternalOutput").ap()
    build(nc, *args, out)
    r = _run(nc, [arrays], core_ids=[0])
    return r.results[0]["out_0_dram"]
```
